# Optimizing a Trainium2 kernel written in Bass

```python
import numpy as np
import jax
import jax.numpy as jnp

def _softmax(x, axis=-1):
    return jax.nn.softmax(x, axis=axis)

def _gelu(x):
    return jax.nn.gelu(x, approximate=True)

def _silu(x):
    return jax.nn.silu(x)

def _sigmoid(x):
    return jax.nn.sigmoid(x)

def _layernorm(x, axis=-1, eps=1e-05):
    m = jnp.mean(x, axis=axis, keepdims=True)
    v = jnp.var(x, axis=axis, keepdims=True)
    return (x - m) / jnp.sqrt(v + eps)

def _scatter_add(tgt, idx, src, axis=0):
    return tgt.at[idx].add(src)

def _segment_sum(src, seg, n):
    return jax.ops.segment_sum(src, seg, n)
kernel_name = 'mk_adaln_d1_jaxref_r8_e43f67'

def setup_inputs(seed: int=0):
    np.random.seed(seed)
    _w = jnp.asarray

    def _L0_attn_setup():
        import jax, jax.numpy as jnp
        import numpy as np
        EPS = 1e-06
        N_HEADS = 16

        def _heads(t, B, N, H, Dk):
            return t.reshape(B, N, H, Dk).transpose(0, 2, 1, 3)
        key = jax.random.key(seed)
        ks = jax.random.split(key, 5)
        B, N, D = (64, 64, 128)
        x = jax.random.normal(ks[0], (B, N, D), dtype=jnp.float32)
        s = 0.02
        W_q = jax.random.normal(ks[1], (D, D), dtype=jnp.float32) * s
        W_k = jax.random.normal(ks[2], (D, D), dtype=jnp.float32) * s
        W_v = jax.random.normal(ks[3], (D, D), dtype=jnp.float32) * s
        W_o = jax.random.normal(ks[4], (D, D), dtype=jnp.float32) * s
        z = jnp.zeros((D,), dtype=jnp.float32)
        return {'x': x, 'W_q': W_q, 'b_q': z, 'W_k': W_k, 'b_k': z, 'W_v': W_v, 'b_v': z, 'W_o': W_o, 'b_o': z}
    _L0_attn_in = _L0_attn_setup()

    def _L0_ffn_setup():
        import jax, jax.numpy as jnp
        import numpy as np
        B, S, D = (4, 512, 128)
        E, F_EXP = (16, 256)
        F_C = 2.0
        F_SH = 256
        key = jax.random.key(seed)
        ks = jax.random.split(key, 8)
        s = 0.02
        return {'hidden_states': jax.random.normal(ks[0], (B, S, D), jnp.float32), 'gate_w': jax.random.normal(ks[1], (E, D), jnp.float32) * s, 'Wg': jax.random.normal(ks[2], (E, F_EXP, D), jnp.float32) * s, 'Wu': jax.random.normal(ks[3], (E, F_EXP, D), jnp.float32) * s, 'Wd': jax.random.normal(ks[4], (E, D, F_EXP), jnp.float32) * s, 'Ws_g': jax.random.normal(ks[5], (F_SH, D), jnp.float32) * s, 'Ws_u': jax.random.normal(ks[6], (F_SH, D), jnp.float32) * s, 'Ws_d': jax.random.normal(ks[7], (D, F_SH), jnp.float32) * s}
    _L0_ffn_in = _L0_ffn_setup()
    _L0_c = _w((lambda *s: np.random.randn(*s).astype(np.float32) * 0.05)(2, 128))
    _L0_wmod = _w((lambda *s: np.random.randn(*s).astype(np.float32) * 0.05)(128, 6 * 128) * 128 ** (-0.5))
    _d = {'L0_attn_x': _L0_attn_in['x'], 'L0_attn_W_q': _L0_attn_in['W_q'], 'L0_attn_b_q': _L0_attn_in['b_q'], 'L0_attn_W_k': _L0_attn_in['W_k'], 'L0_attn_b_k': _L0_attn_in['b_k'], 'L0_attn_W_v': _L0_attn_in['W_v'], 'L0_attn_b_v': _L0_attn_in['b_v'], 'L0_attn_W_o': _L0_attn_in['W_o'], 'L0_attn_b_o': _L0_attn_in['b_o'], 'L0_ffn_gate_w': _L0_ffn_in['gate_w'], 'L0_ffn_Wg': _L0_ffn_in['Wg'], 'L0_ffn_Wu': _L0_ffn_in['Wu'], 'L0_ffn_Wd': _L0_ffn_in['Wd'], 'L0_ffn_Ws_g': _L0_ffn_in['Ws_g'], 'L0_ffn_Ws_u': _L0_ffn_in['Ws_u'], 'L0_ffn_Ws_d': _L0_ffn_in['Ws_d'], 'L0_c': _L0_c, 'L0_wmod': _L0_wmod}
    _x0 = _d['L0_attn_x']
    _d['L0_attn_x'] = jax.random.normal(jax.random.fold_in(jax.random.key(seed), 1), (2, 1024, 128), dtype=_x0.dtype)
    del _x0
    return _d

def reference(L0_attn_x, L0_attn_W_q, L0_attn_b_q, L0_attn_W_k, L0_attn_b_k, L0_attn_W_v, L0_attn_b_v, L0_attn_W_o, L0_attn_b_o, L0_ffn_gate_w, L0_ffn_Wg, L0_ffn_Wu, L0_ffn_Wd, L0_ffn_Ws_g, L0_ffn_Ws_u, L0_ffn_Ws_d, L0_c, L0_wmod):

    def _L0_attn_ref(x, W_q, b_q, W_k, b_k, W_v, b_v, W_o, b_o):
        import jax, jax.numpy as jnp
        import numpy as np
        EPS = 1e-06
        N_HEADS = 16

        def _heads(t, B, N, H, Dk):
            return t.reshape(B, N, H, Dk).transpose(0, 2, 1, 3)
        B, N, Dm = x.shape
        H = N_HEADS
        Dk = Dm // H
        q = _heads(x @ W_q.T + b_q, B, N, H, Dk)
        k = _heads(x @ W_k.T + b_k, B, N, H, Dk)
        v = _heads(x @ W_v.T + b_v, B, N, H, Dk)
        dec = jnp.exp(-jnp.arange(N, dtype=jnp.float32) / N)[None, None, :, None]
        qf = jax.nn.relu(q) * dec
        kf = jax.nn.relu(k) * dec
        KV = jnp.einsum('bhnd,bhne->bhde', kf, v)
        Ksum = kf.sum(axis=2)
        denom = jnp.einsum('bhnd,bhd->bhn', qf, Ksum) + EPS
        out = jnp.einsum('bhnd,bhde->bhne', qf, KV) / denom[..., None]
        out = out.transpose(0, 2, 1, 3).reshape(B, N, Dm)
        return out @ W_o.T + b_o

    def _L0_ffn_ref(hidden_states, gate_w, Wg, Wu, Wd, Ws_g, Ws_u, Ws_d):
        import jax, jax.numpy as jnp
        import numpy as np
        B, S, D = (4, 512, 128)
        E, F_EXP = (16, 256)
        F_C = 2.0
        F_SH = 256
        b, s, d = hidden_states.shape
        e = gate_w.shape[0]
        cap = int(s * F_C / e)
        logits = jnp.einsum('bsd,ed->bse', hidden_states, gate_w)
        scores = jax.nn.softmax(logits, axis=-1).transpose(0, 2, 1)
        topk_w, topk_idx = jax.lax.top_k(scores, cap)
        x_tok = jnp.take_along_axis(hidden_states[:, None, :, :], topk_idx[..., None], axis=2)
        g = jnp.einsum('becd,efd->becf', x_tok, Wg)
        u = jnp.einsum('becd,efd->becf', x_tok, Wu)
        h = jax.nn.gelu(g, approximate=False) * u
        eo = jnp.einsum('becf,edf->becd', h, Wd) * topk_w[..., None]
        offs = (jnp.arange(b) * s)[:, None, None]
        flat_idx = (topk_idx + offs).reshape(-1)
        flat = jnp.zeros((b * s, d), hidden_states.dtype)
        flat = flat.at[flat_idx].add(eo.reshape(-1, d))
        out = flat.reshape(b, s, d)
        gs = jnp.einsum('bsd,fd->bsf', hidden_states, Ws_g)
        us = jnp.einsum('bsd,fd->bsf', hidden_states, Ws_u)
        shared = jnp.einsum('bsf,df->bsd', jax.nn.gelu(gs, approximate=False) * us, Ws_d)
        return out + shared
    x = L0_attn_x
    mod = (_silu(L0_c) @ L0_wmod).reshape(L0_c.shape[0], 6, 1, -1)
    sa, ca, ga, sb, cb, gb = (mod[:, 0], mod[:, 1], mod[:, 2], mod[:, 3], mod[:, 4], mod[:, 5])
    ga = (2 * (ga >= 0) - 1) * jnp.maximum(jnp.abs(ga), 0.25)
    gb = (2 * (gb >= 0) - 1) * jnp.maximum(jnp.abs(gb), 0.25)
    h = _layernorm(x, axis=-1) * (1 + ca) + sa
    x = x + ga * _L0_attn_ref(h, L0_attn_W_q, L0_attn_b_q, L0_attn_W_k, L0_attn_b_k, L0_attn_W_v, L0_attn_b_v, L0_attn_W_o, L0_attn_b_o)
    h = _layernorm(x, axis=-1) * (1 + cb) + sb
    x = x + gb * _L0_ffn_ref(h, L0_ffn_gate_w, L0_ffn_Wg, L0_ffn_Wu, L0_ffn_Wd, L0_ffn_Ws_g, L0_ffn_Ws_u, L0_ffn_Ws_d)
    return x

_drawn_inputs = setup_inputs


def setup_inputs(seed=0):
    import zlib

    import numpy as np

    out = dict(_drawn_inputs(seed))
    spreads = {'L0_attn_b_q': (0.0, 0.8),
     'L0_attn_b_k': (0.0, 0.8),
     'L0_attn_b_v': (0.0, 0.8),
     'L0_attn_b_o': (0.0, 0.306)}
    factors = {'L0_attn_W_q': 8.0,
     'L0_attn_W_k': 8.0,
     'L0_attn_W_v': 8.0,
     'L0_attn_W_o': 8.0,
     'L0_ffn_gate_w': 8.0,
     'L0_ffn_Wg': 8.0,
     'L0_ffn_Wu': 8.0,
     'L0_ffn_Wd': 8.0,
     'L0_ffn_Ws_g': 8.0,
     'L0_ffn_Ws_u': 8.0,
     'L0_ffn_Ws_d': 8.0}
    for name, (base, spread) in spreads.items():
        noise = np.random.default_rng([zlib.crc32(name.encode()), seed]).standard_normal(out[name].shape)
        drawn = base * np.exp(spread * noise) if base else spread * noise
        out[name] = jnp.asarray(drawn.astype(out[name].dtype))
    for name, factor in factors.items():
        out[name] = (out[name] * factor).astype(out[name].dtype)
    return out
```

```python
from contextlib import ExitStack

import concourse.bass as bass
from concourse import mybir

P = 128
B, N, D = 2, 1024, 128
H = 16
E, F = 16, 256
CAP = 2 * N // E
FT = F // P
TILES = B * N // P
TPB = N // P
GT = 4
GROUPS = TILES // GT
GPB = GROUPS // B
GN = GT * P
HALF = N // 2
QUARTERS = HALF // P
ROUNDS = CAP // 8
ROWS = 2 * B * E
UNITS = 2 * B
WCOLS = 3 * FT * P
LN_EPS = 1e-5

F32 = mybir.dt.float32
F32R = mybir.dt.float32r
U32 = mybir.dt.uint32
ALU = mybir.AluOpType
ACT = mybir.ActivationFunctionType
AX_X = mybir.AxisListType.X

EARLY = {"c": (0, B), "bq": (B, B + 1), "eps": (B + 1, B + 2), "wmod": (B + 2, B + 2 + 6 * D)}
ATTN = {"wq": (0, 128), "wk": (128, 256), "wv": (256, 384), "wo": (384, 512), "bv": (512, 640),
        "bo": (640, 768), "gate": (768, 784)}
CONST = {"ident": (0, 128), "flip": (128, 256), "blocks": (256, 384), "heads": (384, 400),
         "dec": (400, 408), "epsdec": (408, 416)}
MOD_SA, MOD_CA, MOD_GA, MOD_SB, MOD_CB, MOD_GB = range(6)


def adaln_moe_block(nc, x, early, attn, bk_row, const, iota, wexp, out):
    xhat_rows = nc.dram_tensor("xhat_rows", [B * N, D], F32, kind="Internal").ap()
    x_v = x.rearrange("b (t p) d -> p (b t) d", p=P)
    xhat_v = xhat_rows.rearrange("(t p) d -> p t d", p=P)
    out_v = out.rearrange("b (t p) d -> p (b t) d", p=P)

    ctx = ExitStack()
    with ctx:
        def sb(name, shape, dt=F32):
            return ctx.enter_context(nc.sbuf_tensor(name, shape, dt))

        def sem(name):
            return ctx.enter_context(nc.semaphore(name))

        x_sb = sb("x_sb", [P, TILES, D])
        xg = sb("xg", [P, TILES, D])
        early_sb = sb("early_sb", [P, EARLY["wmod"][1]])
        attn_sb = sb("attn_sb", [P, ATTN["gate"][1]])
        const_sb = sb("const_sb", [P, CONST["epsdec"][1]])
        bk_sb = sb("bk_sb", [1, GN])
        ones_row = sb("ones_row", [1, P])
        iota_sb = sb("iota_sb", [P, N])
        wshared = sb("wshared", [P, WCOLS])
        wring = sb("wring", [P, 2, WCOLS])
        exp_c = sb("exp_c", [P, B])
        exp_c1 = sb("exp_c1", [P, B])
        sig_c = sb("sig_c", [P, B])
        silu_c = sb("silu_c", [P, B])
        silu_wide = sb("silu_wide", [P, B, P])
        mod = sb("mod", [P, 6 * B])
        scale_a = sb("scale_a", [P, B])
        scale_b = sb("scale_b", [P, B])
        gb_sign = sb("gb_sign", [P, B])
        gb_turned = sb("gb_turned", [P, B])
        gb_size = sb("gb_size", [P, B])
        gb_col = sb("gb_col", [P, B])
        ga_sign = sb("ga_sign", [P, B, D])
        ga_turned = sb("ga_turned", [P, B, D])
        ga_size = sb("ga_size", [P, B, D])
        ga_row = sb("ga_row", [P, B, D])
        wo_gated = sb("wo_gated", [P, B, D])
        bo_gated = sb("bo_gated", [P, B, D])
        stats = sb("stats", [P, 2 * TILES, 6])
        moments = sb("moments", [P, 2 * TILES, 2])
        std = sb("std", [P, 2 * TILES])
        rstd = sb("rstd", [P, 2 * TILES])
        xhat = sb("xhat", [P, TILES, D])
        hT = sb("hT", [P, TILES, P])
        qT = sb("qT", [P, TILES, P])
        k_sb = sb("k_sb", [P, 2, GT, D])
        v_sb = sb("v_sb", [P, 2, GT, D + 1])
        ksum = sb("ksum", [P, B])
        kv_full = sb("kv_full", [P, B, D])
        kv_heads = sb("kv_heads", [P, B, D + H])
        den = sb("den", [P, 2, GT, H])
        rden = sb("rden", [P, 2, GT, H])
        att = sb("att", [P, 2, GT, D])
        attT = sb("attT", [P, 2, GT, P])
        logits = sb("logits", [P, TILES, E])
        top = sb("top", [P, TILES])
        shifted = sb("shifted", [P, TILES, E])
        expd = sb("expd", [P, TILES, E])
        total = sb("total", [P, TILES])
        rtotal = sb("rtotal", [P, TILES])
        scores = sb("scores", [P, QUARTERS, 2, B, E])
        work = sb("work", [ROWS, HALF])
        best = sb("best", [ROWS, CAP])
        where = sb("where", [ROWS, CAP], U32)
        wheref = sb("wheref", [ROWS, CAP])
        lists = sb("lists", [P, 2, 2, B * E])
        first_wins = sb("first_wins", [P, B * E])
        second_place = sb("second_place", [P, B * E])
        place_gap = sb("place_gap", [P, B * E])
        place_add = sb("place_add", [P, B * E])
        chosen_w = sb("chosen_w", [P, E, B])
        chosen_at = sb("chosen_at", [P, E, B])
        chosen_row = sb("chosen_row", [P, E, B], U32)
        gelu_s = sb("gelu_s", [P, 2, FT, GN])
        up_s = sb("up_s", [P, 2, FT, GN])
        hid_s = sb("hid_s", [P, 2, FT, GN])
        xe = sb("xe", [P, UNITS, D])
        xeT = sb("xeT", [P, UNITS, P])
        gelu_e = sb("gelu_e", [P, UNITS, FT, P])
        hid_e = sb("hid_e", [P, UNITS, FT, P])
        back = sb("back", [P, UNITS, N], F32R)
        eo_hi = sb("eo_hi", [P, UNITS, D], F32R)
        eo_lo = sb("eo_lo", [P, UNITS, D], F32R)
        moeT = sb("moeT", [P, GROUPS, GN])
        y_sb = sb("y_sb", [P, TILES, D])

        def col(t, table, name):
            a, b = table[name]
            return t[:, a:b]

        ident, flip = col(const_sb, CONST, "ident"), col(const_sb, CONST, "flip")
        blocks, heads = col(const_sb, CONST, "blocks"), col(const_sb, CONST, "heads")
        dec, epsdec = col(const_sb, CONST, "dec"), col(const_sb, CONST, "epsdec")
        eps_col = col(early_sb, EARLY, "eps")
        wmod_at = EARLY["wmod"][0]

        def modulation(j, b):
            return mod[:, j * B + b:j * B + b + 1]

        bank = [ctx.enter_context(nc.psum_tensor(f"bank{i}", [P, GN], F32)) for i in range(8)]
        q_ps, k_ps, v_ps = bank[0], bank[1], bank[2]
        kv_ps = (bank[3], bank[0])
        t_ps = (bank[4], bank[5])
        o_ps = ((bank[6], bank[7]), (bank[1], bank[2]))
        y_ps = (bank[0], bank[3])
        mod_ps, ga_ps = bank[6], bank[7]
        acc = bank[0:4]
        hid_ps = bank[4:8]
        merge_ps = bank[4]
        gu_ps = (bank[4], bank[5])
        xeT_ps, eo_ps = bank[6], bank[7]

        x_in = [sem(f"x_in{g}") for g in range(GROUPS)]
        early_in, attn_in, const_in, bk_in = sem("early_in"), sem("attn_in"), sem("const_in"), sem("bk_in")
        iota_in, shared_in = sem("iota_in"), sem("shared_in")
        w_in = [sem(f"w_in{s}") for s in range(2)]
        rows_out = sem("rows_out")
        rows_in = [sem(f"rows_in{u}") for u in range(UNITS)]
        y_out = sem("y_out")

        ones_set, vones_set = sem("ones_set"), sem("vones_set")
        exp_c_done, silu_steps = sem("exp_c_done"), sem("silu_steps")
        mod_mm, mod_steps = sem("mod_mm"), sem("mod_steps")
        xg_done = sem("xg_done")
        stats_done, moments_done = sem("stats_done"), sem("moments_done")
        std_done, rstd_done, xhat_done = sem("std_done"), sem("rstd_done"), sem("xhat_done")
        xT_mm, hT_done = sem("xT_mm"), sem("hT_done")
        q_mm, k_mm, v_mm, kv_mm = sem("q_mm"), sem("k_mm"), sem("v_mm"), sem("kv_mm")
        q_done, k_done, v_done = sem("q_done"), sem("k_done"), sem("v_done")
        ksum_done, kvfull_done, kv_done = sem("ksum_done"), sem("kvfull_done"), sem("kv_done")
        o_mm, den_done, rden_done, att_done = sem("o_mm"), sem("den_done"), sem("rden_done"), sem("att_done")
        attT_mm, attT_done = sem("attT_mm"), sem("attT_done")
        y_mm, x1_done = sem("y_mm"), sem("x1_done")
        logit_mm, logit_done = sem("logit_mm"), sem("logit_done")
        soft_steps, expd_done = sem("soft_steps"), sem("expd_done")
        scoresT_mm, work_done = sem("scoresT_mm"), sem("work_done")
        sort_steps, lists_mm, merge_steps, flip_mm = sem("sort_steps"), sem("lists_mm"), sem("merge_steps"), sem("flip_mm")
        sg_mm, su_mm = sem("sg_mm"), sem("su_mm")
        sgelu_done, sup_done, shid_done, sdown_mm = sem("sgelu_done"), sem("sup_done"), sem("shid_done"), sem("sdown_mm")
        xeT_mm, xeT_done, gu_mm = sem("xeT_mm"), sem("xeT_done"), sem("gu_mm")
        gelu_done, hid_done, eo_mm = sem("gelu_done"), sem("hid_done"), sem("eo_mm")
        hi_done, lo_done, back_done, back_mm = sem("hi_done"), sem("lo_done"), sem("back_done"), sem("back_mm")
        moe_done, moeT_mm, y_done = sem("moe_done"), sem("moeT_mm"), sem("y_done")

        MOD_COPIED, MOD_SCALES, GA_ROW, GATED = 1, 3, 7, 9
        GB_COL = 13
        LISTED, MERGED = 1, 9

        block = ctx.enter_context(nc.Block())

        @block.sync
        def _(sp):
            sp.dma_start(x_sb[:, 0:GT, :], x_v[:, 0:GT, :]).then_inc(x_in[0], 16)
            sp.dma_start(early_sb[:, :], early).then_inc(early_in, 16)
            sp.dma_start(const_sb[:, :], const).then_inc(const_in, 16)
            sp.dma_start(attn_sb[:, :], attn).then_inc(attn_in, 16)
            sp.dma_start(bk_sb[:, :], bk_row).then_inc(bk_in, 16)
            for g in range(1, GROUPS):
                sp.dma_start(x_sb[:, g * GT:(g + 1) * GT, :], x_v[:, g * GT:(g + 1) * GT, :]).then_inc(x_in[g], 16)
            sp.dma_start(wshared[:, :], wexp[E, :, :]).then_inc(shared_in, 16)
            sp.dma_start(iota_sb[:, :], iota).then_inc(iota_in, 16)
            for s in range(2):
                sp.dma_start(wring[:, s, :], wexp[s, :, :]).then_inc(w_in[s], 16)
            for g in range(GROUPS):
                sp.wait_ge(xhat_done, TILES + (g + 1) * GT)
                sp.dma_start(xhat_v[:, g * GT:(g + 1) * GT, :], xhat[:, g * GT:(g + 1) * GT, :]).then_inc(rows_out, 16)
            with sp.Fori(1, E // 2) as i:
                for s in range(2):
                    sp.wait_ge(eo_mm, (i - 1) * UNITS + B * (s + 1))
                    sp.dma_start(wring[:, s, :], wexp[bass.ds(i * 2 + s, 1), :, :].rearrange("a p n -> p (a n)")).then_inc(w_in[s], 16)
            for g in range(GROUPS):
                sp.wait_ge(y_done, g + 1)
                sp.dma_start(out_v[:, g * GT:(g + 1) * GT, :], y_sb[:, g * GT:(g + 1) * GT, :]).then_inc(y_out, 16)
            sp.wait_ge(y_out, 16 * GROUPS)

        @block.gpsimd
        def _(pool):
            pool.memset(ones_row[:, :], 1.0).then_inc(ones_set, 1)
            for g in range(GROUPS):
                pool.wait_ge(x_in[g], 16)
                if g == 0:
                    pool.wait_ge(mod_steps, GATED)
                pool.tensor_tensor(xg[:, g * GT:(g + 1) * GT, :], x_sb[:, g * GT:(g + 1) * GT, :],
                                   bo_gated[:, g // GPB:g // GPB + 1, :].to_broadcast([P, GT, D]),
                                   op=ALU.add).then_inc(xg_done, 1)
            for c in range(GROUPS):
                for f in range(FT):
                    n = c * FT + f + 1
                    pool.wait_ge(sgelu_done, n)
                    pool.wait_ge(sup_done, n)
                    if c >= 2:
                        pool.wait_ge(sdown_mm, c - 1)
                    pool.tensor_tensor(hid_s[:, c % 2, f, :], gelu_s[:, c % 2, f, :], up_s[:, c % 2, f, :],
                                       op=ALU.mult).then_inc(shid_done, 1)
            pool.wait_ge(rows_out, 16 * GROUPS)
            pool.wait_ge(merge_steps, MERGED)

            for e in range(E):
                for b in range(B):
                    n = e * B + b
                    if n >= UNITS:
                        pool.wait_ge(xeT_mm, n - UNITS + 1)
                    pool.indirect_dma_start(
                        out=xe[:, n % UNITS, :], out_offset=None, in_=xhat_rows,
                        in_offset=bass.IndirectOffsetOnAxis(ap=chosen_row[:, e, b:b + 1], axis=0))\
                        .then_inc(rows_in[n % UNITS], 16)

        @block.scalar
        def _(act):
            act.wait_ge(early_in, 16)
            act.activation(exp_c[:, :], col(early_sb, EARLY, "c"), ACT.Exp, scale=-1.0).then_inc(exp_c_done, 1)

            def norm_std(n):
                act.wait_ge(moments_done, (n + 1) * GT)
                act.activation(std[:, n * GT:(n + 1) * GT], moments[:, n * GT:(n + 1) * GT, 1], ACT.Sqrt,
                               bias=eps_col).then_inc(std_done, 1)

            def modulated(n, scale, shift):
                g = n % GROUPS
                act.wait_ge(xT_mm, n + 1)
                act.activation(hT[:, g * GT:(g + 1) * GT, :], t_ps[t_slot(n)][:, :].rearrange("p (t q) -> p t q", q=P),
                               ACT.Identity, scale=scale[:, g // GPB:g // GPB + 1],
                               bias=modulation(shift, g // GPB)).then_inc(hT_done, 1)

            norm_std(0)
            for g in range(GROUPS):
                if g + 1 < GROUPS:
                    norm_std(g + 1)
                if g == 0:
                    act.wait_ge(mod_steps, MOD_SCALES)
                modulated(g, scale_a, MOD_SA)
                act.wait_ge(q_mm, g + 1)
                act.activation(qT[:, g * GT:(g + 1) * GT, :], q_ps[:, :].rearrange("p (t q) -> p t q", q=P), ACT.Relu,
                               bias=col(early_sb, EARLY, "bq")).then_inc(q_done, 1)
                act.wait_ge(k_mm, g + 1)
                if g >= 2:
                    act.wait_ge(kv_mm, g - 1)
                act.activation(k_sb[:, g % 2, :, :], k_ps[:, :].rearrange("p (t q) -> p t q", q=D), ACT.Relu).then_inc(k_done, 1)
            def attention_out(g):
                act.wait_ge(attT_mm, g + 1)
                if g >= 2:
                    act.wait_ge(y_mm, g - 1)
                act.activation(attT[:, g % 2, :, :], t_ps[1][:, :].rearrange("p (t q) -> p t q", q=P), ACT.Copy).then_inc(attT_done, 1)

            attention_out(0)
            for g in range(GROUPS):
                if g + 1 < GROUPS:
                    attention_out(g + 1)
                norm_std(GROUPS + g)
                modulated(GROUPS + g, scale_b, MOD_SB)
                act.wait_ge(logit_mm, g + 1)
                act.activation(logits[:, g * GT:(g + 1) * GT, :],
                               t_ps[0][:, 0:GT * E].rearrange("p (t e) -> p t e", e=E), ACT.Copy).then_inc(logit_done, 1)
            act.wait_ge(soft_steps, 2)
            act.activation(expd[:, :, :], shifted[:, :, :], ACT.Exp).then_inc(expd_done, 1)
            act.wait_ge(scoresT_mm, 1)
            act.activation(work[:, :], t_ps[0][0:ROWS, :], ACT.Copy).then_inc(work_done, 1)
            for c in range(GROUPS):
                for f in range(FT):
                    n = c * FT + f + 1
                    act.wait_ge(sg_mm, n)
                    if c >= 2:
                        act.wait_ge(shid_done, n - 2 * FT)
                    act.activation(gelu_s[:, c % 2, f, :], hid_ps[f][:, :], ACT.Gelu).then_inc(sgelu_done, 1)
                    act.wait_ge(su_mm, n)
                    act.activation(up_s[:, c % 2, f, :], hid_ps[FT + f][:, :], ACT.Copy).then_inc(sup_done, 1)

            def evacuate_x(i, u):
                act.wait_ge(xeT_mm, i * UNITS + u + 1)
                act.activation(xeT[:, u, :], xeT_ps[:, u * P:(u + 1) * P], ACT.Identity,
                               scale=scale_b[:, u % B:u % B + 1], bias=modulation(MOD_SB, u % B)).then_inc(xeT_done, 1)

            def gelu(i, u):
                act.wait_ge(gu_mm, i * UNITS + u + 1)
                act.activation(gelu_e[:, u, :, :], gu_ps[u % 2][:, 0:F].rearrange("p (f q) -> p f q", q=P),
                               ACT.Gelu).then_inc(gelu_done, 1)

            def weigh(i, u):
                act.wait_ge(eo_mm, i * UNITS + u + 1)
                if not (isinstance(i, int) and i == 0):
                    act.wait_ge(back_mm, (i - 1) * UNITS + u + 1)
                act.activation(eo_hi[:, u, :], eo_ps[:, u * D:(u + 1) * D], ACT.Copy,
                               scale=chosen_w[:, bass.ds(i * 2 + u // B, 1), u % B]).then_inc(hi_done, 1)

            def body(i, first=False, last=False):
                for u in range(UNITS):
                    if u + 1 < UNITS:
                        evacuate_x(i, u + 1)
                    elif not last:
                        evacuate_x(i + 1, 0)
                    gelu(i, u)
                    if u:
                        weigh(i, u - 1)
                    elif not first:
                        weigh(i - 1, UNITS - 1)

            act.wait_ge(merge_steps, MERGED)
            evacuate_x(0, 0)
            body(0, first=True)
            with act.Fori(1, E // 2 - 1) as i:
                body(i)
            body(E // 2 - 1, last=True)
            weigh(E // 2 - 1, UNITS - 1)
            for g in range(GROUPS):
                act.wait_ge(back_mm, UNITS * E // 2)
                act.activation(moeT[:, g, :], acc[g][:, :], ACT.Copy, scale=gb_col[:, g // GPB:g // GPB + 1]).then_inc(moe_done, 1)

        @block.vector
        def _(dve):
            def norm_stats(n, src):
                g = n % GROUPS
                for t in range(GT):
                    dve.bn_stats(stats[:, n * GT + t, :], src[:, g * GT + t, :]).then_inc(stats_done, 1)
                for t in range(GT):
                    dve.wait_ge(stats_done, n * GT + t + 1)
                    dve.bn_aggr(moments[:, n * GT + t, :], stats[:, n * GT + t, :]).then_inc(moments_done, 1)

            def normalise(n, src):
                g = n % GROUPS
                dve.wait_ge(std_done, n + 1)
                dve.reciprocal(rstd[:, n * GT:(n + 1) * GT], std[:, n * GT:(n + 1) * GT]).then_inc(rstd_done, 1)
                dve.wait_ge(rstd_done, n + 1)
                for t in range(GT):
                    if n >= GROUPS and t == 0:
                        dve.wait_ge(xT_mm, g + 1)
                    m = n * GT + t
                    dve.tensor_scalar(xhat[:, g * GT + t, :], src[:, g * GT + t, :], moments[:, m, 0:1], rstd[:, m:m + 1],
                                      op0=ALU.subtract, op1=ALU.mult).then_inc(xhat_done, 1)

            dve.wait_ge(x_in[0], 16)
            norm_stats(0, x_sb)
            dve.wait_ge(exp_c_done, 1)
            dve.tensor_scalar_add(exp_c1[:, :], exp_c[:, :], 1.0).then_inc(silu_steps, 1)
            dve.wait_ge(silu_steps, 1)
            dve.reciprocal(sig_c[:, :], exp_c1[:, :]).then_inc(silu_steps, 1)
            dve.wait_ge(silu_steps, 2)
            dve.tensor_tensor(silu_c[:, :], col(early_sb, EARLY, "c"), sig_c[:, :], op=ALU.mult).then_inc(silu_steps, 1)
            dve.wait_ge(silu_steps, 3)
            dve.tensor_copy(silu_wide[:, :, :], silu_c[:, :].unsqueeze(2).to_broadcast([P, B, P])).then_inc(silu_steps, 1)
            normalise(0, x_sb)
            dve.wait_ge(x_in[1], 16)
            norm_stats(1, x_sb)
            dve.wait_ge(mod_mm, 1)
            dve.tensor_copy(mod[:, :], mod_ps[:, 0:6 * B]).then_inc(mod_steps, 1)
            dve.wait_ge(mod_steps, MOD_COPIED)
            dve.tensor_scalar_add(scale_a[:, :], mod[:, MOD_CA * B:(MOD_CA + 1) * B], 1.0).then_inc(mod_steps, 1)
            dve.tensor_scalar_add(scale_b[:, :], mod[:, MOD_CB * B:(MOD_CB + 1) * B], 1.0).then_inc(mod_steps, 1)

            def guarded(size, turned, sign, gate, raw):
                n = guarded.done
                dve.tensor_scalar(sign, raw, 0.0, 2.0, op0=ALU.is_ge, op1=ALU.mult).then_inc(mod_steps, 1)
                dve.tensor_scalar(turned, raw, -1.0, 0.25, op0=ALU.mult, op1=ALU.max).then_inc(mod_steps, 1)
                dve.wait_ge(mod_steps, n + 2)
                dve.scalar_tensor_tensor(size, raw, 0.25, turned, op0=ALU.max, op1=ALU.max).then_inc(mod_steps, 1)
                dve.wait_ge(mod_steps, n + 3)
                dve.scalar_tensor_tensor(gate, sign, -1.0, size, op0=ALU.add, op1=ALU.mult).then_inc(mod_steps, 1)
                guarded.done = n + 4

            guarded.done = MOD_SCALES
            dve.wait_ge(mod_mm, 2)
            guarded(ga_size[:, :, :], ga_turned[:, :, :], ga_sign[:, :, :], ga_row[:, :, :],
                    ga_ps[:, 0:B * D].rearrange("p (b d) -> p b d", b=B))
            dve.wait_ge(mod_steps, GA_ROW)
            dve.wait_ge(attn_in, 16)
            for name, gated in (("wo", wo_gated), ("bo", bo_gated)):
                dve.tensor_tensor(gated[:, :, :], ga_row[:, :, :],
                                  col(attn_sb, ATTN, name).unsqueeze(1).to_broadcast([P, B, D]),
                                  op=ALU.mult).then_inc(mod_steps, 1)
            guarded.done = GATED
            guarded(gb_size[:, :], gb_turned[:, :], gb_sign[:, :], gb_col[:, :], mod[:, MOD_GB * B:(MOD_GB + 1) * B])

            def heads_of(b):
                dve.wait_ge(kv_mm, (b + 1) * GPB)
                dve.tensor_copy(ksum[:, b:b + 1], kv_ps[b][:, D:D + 1]).then_inc(ksum_done, 1)
                dve.wait_ge(ksum_done, b + 1)
                dve.scalar_tensor_tensor(kv_full[:, b, :], col(attn_sb, ATTN, "bv"), ksum[:, b:b + 1],
                                         kv_ps[b][:, 0:D], op0=ALU.mult, op1=ALU.add).then_inc(kvfull_done, 1)
                dve.tensor_scalar_mul(kv_heads[:, b, D:D + H], heads, ksum[:, b:b + 1]).then_inc(kv_done, 1)
                dve.wait_ge(kvfull_done, b + 1)
                dve.tensor_tensor(kv_heads[:, b, 0:D], kv_full[:, b, :], blocks, op=ALU.mult).then_inc(kv_done, 1)

            dve.wait_ge(const_in, 16)
            for g in range(GROUPS):
                if g + 1 < GROUPS:
                    normalise(g + 1, x_sb)
                if g + 2 < GROUPS:
                    dve.wait_ge(x_in[g + 2], 16)
                    norm_stats(g + 2, x_sb)
                if g >= 2:
                    dve.wait_ge(kv_mm, g - 1)
                dec_g = dec[:, (g % GPB) * GT:(g % GPB + 1) * GT].unsqueeze(2)
                dve.tensor_copy(v_sb[:, g % 2, :, D:D + 1], dec_g).then_inc(v_done, 1)
                dve.wait_ge(v_mm, g + 1)
                dve.tensor_tensor(v_sb[:, g % 2, :, 0:D], v_ps[:, :].rearrange("p (t q) -> p t q", q=D),
                                  dec_g.to_broadcast([P, GT, D]), op=ALU.mult).then_inc(v_done, 1)
                if g == GPB:
                    heads_of(0)
            heads_of(1)

            def divide(g):
                s = g % 2
                dve.wait_ge(o_mm, g + 1)
                if g >= 2:
                    dve.wait_ge(attT_mm, g - 1)
                eps_g = epsdec[:, (g % GPB) * GT:(g % GPB + 1) * GT]
                for half in range(2):
                    o = o_ps[s][half][:, :].rearrange("p (t q) -> p t q", q=256)
                    dve.tensor_tensor(den[:, s, 2 * half:2 * half + 2, :], o[:, :, D:D + H],
                                      eps_g[:, 2 * half:2 * half + 2].unsqueeze(2).to_broadcast([P, 2, H]),
                                      op=ALU.add).then_inc(den_done, 1)
                dve.wait_ge(den_done, 2 * g + 2)
                dve.reciprocal(rden[:, s, :, :], den[:, s, :, :]).then_inc(rden_done, 1)
                dve.wait_ge(rden_done, g + 1)
                for half in range(2):
                    o = o_ps[s][half][:, :].rearrange("p (t q) -> p t q", q=256)
                    dve.tensor_tensor(att[:, s, 2 * half:2 * half + 2, :].rearrange("p t (h k) -> p t h k", h=H),
                                      o[:, :, 0:D].rearrange("p t (h k) -> p t h k", h=H),
                                      rden[:, s, 2 * half:2 * half + 2, :].unsqueeze(3).to_broadcast([P, 2, H, D // H]),
                                      op=ALU.mult).then_inc(att_done, 1)

            def residual(g):
                dve.wait_ge(y_mm, g + 1)
                dve.wait_ge(xg_done, g + 1)
                dve.tensor_tensor(xg[:, g * GT:(g + 1) * GT, :], xg[:, g * GT:(g + 1) * GT, :],
                                  y_ps[g % 2][:, :].rearrange("p (t q) -> p t q", q=D), op=ALU.add).then_inc(x1_done, 1)
                dve.wait_ge(x1_done, g + 1)

            divide(0)
            for g in range(GROUPS):
                if g + 1 < GROUPS:
                    divide(g + 1)
                residual(g)
                norm_stats(GROUPS + g, xg)
                normalise(GROUPS + g, xg)

            dve.wait_ge(logit_done, GROUPS)
            dve.tensor_reduce(top[:, :], logits[:, :, :], axis=AX_X, op=ALU.max).then_inc(soft_steps, 1)
            dve.wait_ge(soft_steps, 1)
            dve.tensor_tensor(shifted[:, :, :], logits[:, :, :], top[:, :].unsqueeze(2).to_broadcast([P, TILES, E]),
                              op=ALU.subtract).then_inc(soft_steps, 1)
            dve.wait_ge(expd_done, 1)
            dve.tensor_reduce(total[:, :], expd[:, :, :], axis=AX_X, op=ALU.add).then_inc(soft_steps, 1)
            dve.wait_ge(soft_steps, 3)
            dve.reciprocal(rtotal[:, :], total[:, :]).then_inc(soft_steps, 1)
            dve.wait_ge(soft_steps, 4)
            for b in range(B):
                for h in range(2):
                    t0 = b * TPB + h * QUARTERS
                    dve.tensor_tensor(scores[:, :, h, b, :], expd[:, t0:t0 + QUARTERS, :],
                                      rtotal[:, t0:t0 + QUARTERS].unsqueeze(2).to_broadcast([P, QUARTERS, E]),
                                      op=ALU.mult).then_inc(soft_steps, 1)
            dve.wait_ge(work_done, 1)
            for r in range(ROUNDS):
                at = slice(8 * r, 8 * r + 8)
                if r:
                    dve.wait_ge(sort_steps, 3 * r)
                dve.max(best[:, at], work[:, :]).then_inc(sort_steps, 1)
                dve.wait_ge(sort_steps, 3 * r + 1)
                dve.max_index(where[:, at], best[:, at], work[:, :]).then_inc(sort_steps, 1)
                dve.match_replace(work[:, :], best[:, at], work[:, :], -1.0).then_inc(sort_steps, 1)
            dve.wait_ge(sort_steps, 3 * ROUNDS - 1)
            dve.tensor_copy(wheref[:, :], where[:, :]).then_inc(sort_steps, 1)
            BE = B * E
            dve.wait_ge(lists_mm, 1)
            dve.tensor_copy(lists[:, :, :, :], merge_ps[:, 0:4 * BE].rearrange("p (k h r) -> p k h r", k=2, h=2))\
                .then_inc(merge_steps, 1)
            dve.wait_ge(flip_mm, 1)
            flipped = merge_ps[:, 4 * BE:6 * BE].rearrange("p (k r) -> p k r", k=2)
            dve.tensor_tensor(first_wins[:, :], lists[:, 0, 0, :], flipped[:, 0, :], op=ALU.is_ge).then_inc(merge_steps, 1)
            dve.tensor_tensor(chosen_w[:, :, :].rearrange("p e b -> p b e"), lists[:, 0, 0, :].rearrange("p (b e) -> p b e", b=B),
                              flipped[:, 0, :].rearrange("p (b e) -> p b e", b=B), op=ALU.max).then_inc(merge_steps, 1)
            dve.tensor_scalar_add(second_place[:, :], flipped[:, 1, :], float(HALF)).then_inc(merge_steps, 1)
            dve.wait_ge(merge_steps, LISTED + 3)
            dve.tensor_tensor(place_gap[:, :], lists[:, 1, 0, :], second_place[:, :], op=ALU.subtract).then_inc(merge_steps, 1)
            dve.wait_ge(merge_steps, LISTED + 4)
            dve.tensor_tensor(place_add[:, :], place_gap[:, :], first_wins[:, :], op=ALU.mult).then_inc(merge_steps, 1)
            dve.wait_ge(merge_steps, LISTED + 5)
            dve.tensor_tensor(chosen_at[:, :, :].rearrange("p e b -> p b e"), second_place[:, :].rearrange("p (b e) -> p b e", b=B),
                              place_add[:, :].rearrange("p (b e) -> p b e", b=B), op=ALU.add).then_inc(merge_steps, 1)
            dve.wait_ge(merge_steps, LISTED + 6)
            for b in range(B):
                dve.tensor_scalar_add(chosen_row[:, :, b], chosen_at[:, :, b], float(b * N)).then_inc(merge_steps, 1)

            def way_back(i, u):
                if not (isinstance(i, int) and i == 0):
                    dve.wait_ge(back_mm, (i - 1) * UNITS + u + 1)
                dve.tensor_scalar(back[:, u, :], iota_sb[:, :], chosen_at[:, bass.ds(i * 2 + u // B, 1), u % B], None,
                                  op0=ALU.is_equal).then_inc(back_done, 1)

            def hidden(i, u):
                dve.wait_ge(gelu_done, i * UNITS + u + 1)
                dve.tensor_tensor(hid_e[:, u, :, :], gelu_e[:, u, :, :], gu_ps[u % 2][:, F:2 * F].rearrange("p (f q) -> p f q", q=P),
                                  op=ALU.mult).then_inc(hid_done, 1)

            def low_half(i, u):
                dve.wait_ge(hi_done, i * UNITS + u + 1)
                dve.scalar_tensor_tensor(eo_lo[:, u, :], eo_ps[:, u * D:(u + 1) * D],
                                         chosen_w[:, bass.ds(i * 2 + u // B, 1), u % B],
                                         eo_hi[:, u, :].bitcast(F32), op0=ALU.mult, op1=ALU.subtract).then_inc(lo_done, 1)

            def body(i, first=False):
                for u in range(UNITS):
                    way_back(i, u)
                    hidden(i, u)
                    if u:
                        low_half(i, u - 1)
                    elif not first:
                        low_half(i - 1, UNITS - 1)

            dve.wait_ge(iota_in, 16)
            dve.wait_ge(merge_steps, MERGED)
            body(0, first=True)
            with dve.Fori(1, E // 2) as i:
                body(i)
            low_half(E // 2 - 1, UNITS - 1)
            for g in range(GROUPS):
                dve.wait_ge(moeT_mm, g + 1)
                dve.tensor_tensor(y_sb[:, g * GT:(g + 1) * GT, :], xg[:, g * GT:(g + 1) * GT, :],
                                  bank[4 + g][:, :].rearrange("p (t q) -> p t q", q=D), op=ALU.add).then_inc(y_done, 1)

        @block.tensor
        def _(pe):
            pe.wait_ge(silu_steps, 3)
            pe.wait_ge(early_in, 16)
            for j in range(6):
                last = pe.matmul(mod_ps[:, j * B:(j + 1) * B], early_sb[:, wmod_at + j * D:wmod_at + (j + 1) * D],
                                 silu_c[:, :], start=True, stop=True)
            last.then_inc(mod_mm, 1)
            pe.wait_ge(silu_steps, 4)
            for b in range(B):
                at = wmod_at + MOD_GA * D
                last = pe.matmul(ga_ps[:, b * D:(b + 1) * D], silu_wide[:, b, :], early_sb[:, at:at + D], start=True, stop=True)
            last.then_inc(mod_mm, 1)

            def transposes(n):
                g = n % GROUPS
                pe.wait_ge(xhat_done, (n + 1) * GT)
                for t in range(GT):
                    last = pe.transpose(t_ps[t_slot(n)][:, t * P:(t + 1) * P], xhat[:, g * GT + t, :], ident)
                last.then_inc(xT_mm, 1)

            pe.wait_ge(const_in, 16)
            transposes(0)
            pe.wait_ge(attn_in, 16)
            pe.wait_ge(bk_in, 16)
            pe.wait_ge(ones_set, 1)

            def sum_kv(g):
                pe.wait_ge(k_done, g + 1)
                pe.wait_ge(v_done, 2 * g + 2)
                if g == GPB:
                    pe.wait_ge(q_done, GROUPS)
                for t in range(GT):
                    n = (g % GPB) * GT + t
                    last = pe.matmul(kv_ps[g // GPB][:, 0:D + 1], k_sb[:, g % 2, t, :], v_sb[:, g % 2, t, :],
                                     start=n == 0, stop=n == TPB - 1)
                last.then_inc(kv_mm, 1)

            for g in range(GROUPS):
                if g + 1 < GROUPS:
                    if g >= 1:
                        pe.wait_ge(hT_done, g)
                    transposes(g + 1)
                pe.wait_ge(hT_done, g + 1)
                hT_g = hT[:, g * GT:(g + 1) * GT, :]
                if g:
                    pe.wait_ge(q_done, g)
                pe.matmul(q_ps[:, :].rearrange("p (t q) -> p t q", q=P), col(attn_sb, ATTN, "wq"), hT_g,
                          start=True, stop=True).then_inc(q_mm, 1)
                if g:
                    pe.wait_ge(k_done, g)
                pe.matmul(k_ps[:, :], ones_row[:, :], bk_sb[:, :], start=True, stop=False)
                for t in range(GT):
                    last = pe.matmul(k_ps[:, t * D:(t + 1) * D], hT[:, g * GT + t, :], col(attn_sb, ATTN, "wk"),
                                     start=False, stop=t == GT - 1)
                last.then_inc(k_mm, 1)
                if g:
                    pe.wait_ge(v_done, 2 * g)
                for t in range(GT):
                    last = pe.matmul(v_ps[:, t * D:(t + 1) * D], hT[:, g * GT + t, :], col(attn_sb, ATTN, "wv"),
                                     start=True, stop=True)
                last.then_inc(v_mm, 1)
                if g:
                    sum_kv(g - 1)
            sum_kv(GROUPS - 1)

            def attend(g):
                b = g // GPB
                if g % GPB == 0:
                    pe.wait_ge(kv_done, 2 * b + 2)
                pe.wait_ge(q_done, g + 1)
                if g == 0:
                    pe.wait_ge(mod_steps, GATED)
                if g == 1:
                    pe.wait_ge(k_done, GROUPS)
                    pe.wait_ge(v_done, 2 * GROUPS)
                if g >= 2:
                    pe.wait_ge(att_done, 2 * g - 2)
                for t in range(GT):
                    o = o_ps[g % 2][t // 2]
                    at = (t % 2) * 256
                    last = pe.matmul(o[:, at:at + D + H], qT[:, g * GT + t, :], kv_heads[:, b, :], start=True, stop=True)
                last.then_inc(o_mm, 1)

            def project(g):
                pe.wait_ge(att_done, 2 * g + 2)
                if g == 0:
                    pe.wait_ge(hT_done, GROUPS)
                else:
                    pe.wait_ge(attT_done, g)
                for t in range(GT):
                    last = pe.transpose(t_ps[1][:, t * P:(t + 1) * P], att[:, g % 2, t, :], ident)
                last.then_inc(attT_mm, 1)
                if g + 1 < GROUPS and g >= 1:
                    attend(g + 1)
                pe.wait_ge(attT_done, g + 1)
                if g == 0:
                    pe.wait_ge(kvfull_done, B)
                if g >= 2:
                    pe.wait_ge(x1_done, g - 1)
                for t in range(GT):
                    last = pe.matmul(y_ps[g % 2][:, t * D:(t + 1) * D], attT[:, g % 2, t, :], wo_gated[:, g // GPB, :],
                                     start=True, stop=True)
                last.then_inc(y_mm, 1)

            def route(g):
                pe.wait_ge(hT_done, GROUPS + g + 1)
                for t in range(GT):
                    last = pe.matmul(t_ps[0][:, t * E:(t + 1) * E], hT[:, g * GT + t, :], col(attn_sb, ATTN, "gate"),
                                     start=True, stop=True)
                last.then_inc(logit_mm, 1)

            attend(0)
            attend(1)
            project(0)
            for g in range(GROUPS):
                if g + 1 < GROUPS:
                    project(g + 1)
                if g:
                    pe.wait_ge(logit_done, g)
                transposes(GROUPS + g)
                route(g)

            pe.wait_ge(soft_steps, 4 + 2 * B)
            for q in range(QUARTERS):
                last = pe.transpose(t_ps[0][0:ROWS, q * P:(q + 1) * P], scores[:, q, :, :, :].rearrange("p h b e -> p (h b e)"), ident)
            last.then_inc(scoresT_mm, 1)

            def shared_down(c):
                pe.wait_ge(shid_done, (c + 1) * FT)
                if c == 0:
                    pe.wait_ge(x1_done, GROUPS)
                for f in range(FT):
                    last = pe.matmul(acc[c][:, :], wshared[:, (2 * FT + f) * P:(2 * FT + f + 1) * P], hid_s[:, c % 2, f, :],
                                     start=f == 0, stop=False, skip_group_check=True)
                last.then_inc(sdown_mm, 1)

            pe.wait_ge(shared_in, 16)
            pe.wait_ge(work_done, 1)
            pe.wait_ge(logit_done, GROUPS)
            for c in range(GROUPS):
                for f in range(FT):
                    if c:
                        pe.wait_ge(sgelu_done, (c - 1) * FT + f + 1)
                    pe.matmul(hid_ps[f][:, :], wshared[:, f * P:(f + 1) * P], hT[:, c * GT:(c + 1) * GT, :].rearrange("p t q -> p (t q)"),
                              start=True, stop=True).then_inc(sg_mm, 1)
                    if c:
                        pe.wait_ge(sup_done, (c - 1) * FT + f + 1)
                    pe.matmul(hid_ps[FT + f][:, :], wshared[:, (FT + f) * P:(FT + f + 1) * P],
                              hT[:, c * GT:(c + 1) * GT, :].rearrange("p t q -> p (t q)"), start=True, stop=True).then_inc(su_mm, 1)
                if c:
                    shared_down(c - 1)
            shared_down(GROUPS - 1)

            pe.wait_ge(sort_steps, 3 * ROUNDS + 1)
            BE = B * E
            pe.transpose(merge_ps[:, 0:ROWS], best[:, :], ident[0:ROWS, 0:ROWS])
            pe.transpose(merge_ps[:, ROWS:2 * ROWS], wheref[:, :], ident[0:ROWS, 0:ROWS]).then_inc(lists_mm, 1)
            pe.wait_ge(merge_steps, LISTED)
            for k in range(2):
                last = pe.matmul(merge_ps[:, (4 + k) * BE:(5 + k) * BE], flip, lists[:, k, 1, :], start=True, stop=True)
            last.then_inc(flip_mm, 1)

            def turn(i, u, first=False):
                pe.wait_ge(rows_in[u], 16 * (i + 1))
                if not first:
                    pe.wait_ge(xeT_done, i * UNITS + u)
                pe.transpose(xeT_ps[:, u * P:(u + 1) * P], xe[:, u, :], ident).then_inc(xeT_mm, 1)

            def gate_up(i, u):
                s = u // B
                if u % B == 0:
                    pe.wait_ge(w_in[s], 16 * (i + 1))
                pe.wait_ge(xeT_done, i * UNITS + u + 1)
                for j in range(2 * FT):
                    last = pe.matmul(gu_ps[u % 2][:, j * P:(j + 1) * P], wring[:, s, j * P:(j + 1) * P], xeT[:, u, :],
                                     start=True, stop=True)
                last.then_inc(gu_mm, 1)

            def down(i, u):
                s = u // B
                pe.wait_ge(hid_done, i * UNITS + u + 1)
                if not (isinstance(i, int) and i == 0 and u == 0):
                    pe.wait_ge(lo_done, i * UNITS + u)
                for f in range(FT):
                    last = pe.matmul(eo_ps[:, u * D:(u + 1) * D], hid_e[:, u, f, :],
                                     wring[:, s, (2 * FT + f) * P:(2 * FT + f + 1) * P], start=f == 0, stop=f == FT - 1)
                last.then_inc(eo_mm, 1)

            def put_back(i, u, stop=False):
                b = u % B
                pe.wait_ge(lo_done, i * UNITS + u + 1)
                pe.wait_ge(back_done, i * UNITS + u + 1)
                for k, part in enumerate((eo_hi, eo_lo)):
                    for c in range(GPB):
                        last = pe.matmul(acc[b * GPB + c][:, :], part[:, u, :], back[:, u, c * GN:(c + 1) * GN],
                                         start=False, stop=stop and k == 1, skip_group_check=True)
                last.then_inc(back_mm, 1)

            def body(i, first=False, last=False):
                for u in range(UNITS):
                    if u + 1 < UNITS:
                        turn(i, u + 1)
                    elif not last:
                        turn(i + 1, 0)
                    gate_up(i, u)
                    if u:
                        down(i, u - 1)
                    elif not first:
                        down(i - 1, UNITS - 1)
                    if u >= 2:
                        put_back(i, u - 2, stop=last and u - 2 >= UNITS - B)
                    elif not first:
                        put_back(i - 1, UNITS - 2 + u)

            pe.wait_ge(merge_steps, MERGED)
            turn(0, 0, first=True)
            body(0, first=True)
            with pe.Fori(1, E // 2 - 1) as i:
                body(i)
            n = E // 2 - 1
            body(n, last=True)
            down(n, UNITS - 1)
            put_back(n, UNITS - 2, stop=True)
            put_back(n, UNITS - 1, stop=True)
            for g in range(GROUPS):
                pe.wait_ge(moe_done, g + 1)
                if g == 0:
                    pe.wait_ge(lo_done, UNITS * E // 2)
                for t in range(GT):
                    last = pe.transpose(bank[4 + g][:, t * P:(t + 1) * P], moeT[:, g, t * P:(t + 1) * P], ident)
                last.then_inc(moeT_mm, 1)


def t_slot(n):
    return n % 2 if n < GROUPS else 0


def kernel(L0_attn_x, L0_attn_W_q, L0_attn_b_q, L0_attn_W_k, L0_attn_b_k, L0_attn_W_v, L0_attn_b_v, L0_attn_W_o,
           L0_attn_b_o, L0_ffn_gate_w, L0_ffn_Wg, L0_ffn_Wu, L0_ffn_Wd, L0_ffn_Ws_g, L0_ffn_Ws_u, L0_ffn_Ws_d, L0_c,
           L0_wmod):
    import numpy as np
    import concourse.bacc as bacc
    from concourse.bass_utils import run_bass_kernel_spmd

    f32 = np.float32

    def a(v):
        return np.asarray(v)

    def wide(v):
        return np.broadcast_to(a(v)[None, :], (P, D))

    early = np.concatenate([a(L0_c).T, a(L0_attn_b_q)[:, None], np.full((P, 1), LN_EPS, f32), a(L0_wmod)], axis=1)
    attn = np.concatenate([a(L0_attn_W_q).T, a(L0_attn_W_k).T, a(L0_attn_W_v).T, a(L0_attn_W_o).T,
                           wide(L0_attn_b_v), wide(L0_attn_b_o), a(L0_ffn_gate_w).T], axis=1)
    bk_row = np.tile(a(L0_attn_b_k), GT)[None, :]

    eye = np.eye(P, dtype=f32)
    block_of = np.arange(P) // (D // H)
    decay = np.exp(-np.arange(N, dtype=f32) / N).astype(f32)
    const = np.concatenate([
        eye, eye[:, ::-1], (block_of[:, None] == block_of[None, :]).astype(f32),
        (block_of[:, None] == np.arange(H)[None, :]).astype(f32),
        decay.reshape(TPB, P).T, (f32(1e-6) / decay).astype(f32).reshape(TPB, P).T], axis=1)
    iota = np.tile(np.arange(N, dtype=f32), (P, 1))

    def expert_layout(wg, wu, wd):
        n = wg.shape[0]
        gate_up = np.concatenate([wg.transpose(0, 2, 1), wu.transpose(0, 2, 1)], axis=2)
        down = wd.transpose(0, 2, 1).reshape(n, FT, P, D).transpose(0, 2, 1, 3).reshape(n, P, FT * D)
        return np.concatenate([gate_up, down], axis=2)

    wexp = np.concatenate([expert_layout(a(L0_ffn_Wg), a(L0_ffn_Wu), a(L0_ffn_Wd)),
                           expert_layout(a(L0_ffn_Ws_g)[None], a(L0_ffn_Ws_u)[None], a(L0_ffn_Ws_d)[None])], axis=0)

    arrays = {"in_x": a(L0_attn_x), "in_early": early, "in_attn": attn, "in_bk_row": bk_row, "in_const": const,
              "in_iota": iota, "in_wexp": wexp}
    arrays = {k: np.ascontiguousarray(v) for k, v in arrays.items()}

    nc = bacc.Bacc("TRN2", target_bir_lowering=False, num_devices=1)
    args = [nc.dram_tensor(k, v.shape, F32, kind="ExternalInput").ap() for k, v in arrays.items()]
    args.append(nc.dram_tensor("out_y", (B, N, D), F32, kind="ExternalOutput").ap())
    adaln_moe_block(nc, *args)
    r = run_bass_kernel_spmd(nc, [arrays], core_ids=[0])
    return r.results[0]["out_y"]
```

```python
from contextlib import ExitStack

import concourse.bass as bass
from concourse import mybir

P = 128
B, N, D = 2, 1024, 128
H = 16
E, F = 16, 256
CAP = 2 * N // E
FT = F // P
TILES = B * N // P
TPB = N // P
GT = 4
GROUPS = TILES // GT
GPB = GROUPS // B
GN = GT * P
HALF = N // 2
QUARTERS = HALF // P
ROUNDS = CAP // 8
ROWS = 2 * B * E
UNITS = 2 * B
WCOLS = 3 * FT * P
PAIRS = E // 2
WSLOTS = 4
XSLOTS = 2 * UNITS
AHEAD = 6
LN_EPS = 1e-5

F32 = mybir.dt.float32
F32R = mybir.dt.float32r
U32 = mybir.dt.uint32
ALU = mybir.AluOpType
ACT = mybir.ActivationFunctionType
AX_X = mybir.AxisListType.X

EARLY = {"c": (0, B), "bq": (B, B + 1), "eps": (B + 1, B + 2), "wmod": (B + 2, B + 2 + 6 * D)}
ATTN = {"wq": (0, 128), "wk": (128, 256), "wv": (256, 384), "wo": (384, 512), "bv": (512, 640),
        "bo": (640, 768), "gate": (768, 784)}
CONST = {"ident": (0, 128), "flip": (128, 256), "blocks": (256, 384), "heads": (384, 400),
         "dec": (400, 408), "epsdec": (408, 416)}
MOD_SA, MOD_CA, MOD_GA, MOD_SB, MOD_CB, MOD_GB = range(6)


def adaln_moe_block(nc, x, early, attn, bk_row, const, iota, wexp, out):
    xhat_rows = [nc.dram_tensor(f"xhat_rows{b}", [N, D], F32, kind="Internal").ap() for b in range(B)]
    base_rows = [nc.dram_tensor(f"base_rows{b}", [N, D], F32, kind="Internal").ap() for b in range(B)]
    x_v = x.rearrange("b (t p) d -> p (b t) d", p=P)
    out_v = out.rearrange("b (t p) d -> p (b t) d", p=P)

    ctx = ExitStack()
    with ctx:
        def sb(name, shape, dt=F32):
            return ctx.enter_context(nc.sbuf_tensor(name, shape, dt))

        def sem(name):
            return ctx.enter_context(nc.semaphore(name))

        x_sb = sb("x_sb", [P, TILES, D])
        xg = sb("xg", [P, TILES, D])
        early_sb = sb("early_sb", [P, EARLY["wmod"][1]])
        attn_sb = sb("attn_sb", [P, ATTN["gate"][1]])
        const_sb = sb("const_sb", [P, CONST["epsdec"][1]])
        bk_sb = sb("bk_sb", [2, D + 2])
        bk_high = sb("bk_high", [2, D], F32R)
        bk_rest = sb("bk_rest", [2, D])
        bk_parts = sb("bk_parts", [2, D], F32R)
        ones_two = sb("ones_two", [2, P], F32R)
        ones = sb("ones", [P, GN])
        iota_sb = sb("iota_sb", [P, N])
        wshared = sb("wshared", [P, WCOLS])
        wring = sb("wring", [P, WSLOTS, WCOLS])
        exp_c = sb("exp_c", [P, B])
        exp_c1 = sb("exp_c1", [P, B])
        sig_c = sb("sig_c", [P, B])
        silu_c = sb("silu_c", [P, B])
        mod = sb("mod", [P, 6 * B])
        scale_a = sb("scale_a", [P, B])
        scale_b = sb("scale_b", [P, B])
        gate_turned = sb("gate_turned", [P, 2, B])
        gate_sign = sb("gate_sign", [P, 2, B])
        gate_size = sb("gate_size", [P, 2, B])
        gates = sb("gates", [P, 2, B])
        ga_diag = sb("ga_diag", [P, B, P])
        gb_diag = sb("gb_diag", [P, B, P])
        gb_row = sb("gb_row", [P, B, D])
        wo_gated = sb("wo_gated", [P, B, D])
        bo_gated = sb("bo_gated", [P, B, D])
        stats = sb("stats", [P, 2 * TILES, 6])
        moments = sb("moments", [P, 2 * TILES, 2])
        minus_mean = sb("minus_mean", [P, 2 * TILES])
        std = sb("std", [P, 2 * TILES])
        rstd = sb("rstd", [P, 2 * TILES])
        xhat = sb("xhat", [P, TILES, D])
        hT = sb("hT", [P, TILES, P])
        qT = sb("qT", [P, TILES, P])
        k_sb = sb("k_sb", [P, 2, GT, D])
        v_sb = sb("v_sb", [P, 2, GT, D + 1])
        ksum = sb("ksum", [P, B])
        kv_full = sb("kv_full", [P, B, D])
        kv_heads = sb("kv_heads", [P, B, D + H])
        den = sb("den", [P, 2, GT, H])
        rden = sb("rden", [P, 2, GT, H])
        att = sb("att", [P, 2, GT, D])
        attT = sb("attT", [P, 2, GT, P])
        top = sb("top", [P, TILES])
        shifted = sb("shifted", [P, TILES, E])
        expd = sb("expd", [P, TILES, E])
        total = sb("total", [P, TILES])
        rtotal = sb("rtotal", [P, TILES])
        scores = sb("scores", [P, QUARTERS, 2, B, E])
        work = sb("work", [ROWS, 2, HALF])
        best = sb("best", [ROWS, CAP])
        where = sb("where", [ROWS, CAP], U32)
        wheref = sb("wheref", [ROWS, CAP])
        lists = sb("lists", [P, 2, 2, B * E])
        first_wins = sb("first_wins", [P, B * E])
        second_place = sb("second_place", [P, B * E])
        place_gap = sb("place_gap", [P, B * E])
        place_add = sb("place_add", [P, B * E])
        chosen_w = sb("chosen_w", [P, E, B])
        chosen_at = sb("chosen_at", [P, E, B])
        chosen_row = sb("chosen_row", [P, E, B], U32)
        gelu_s = sb("gelu_s", [P, 2, FT, GN])
        up_s = sb("up_s", [P, 2, FT, GN])
        hid_s = sb("hid_s", [P, 2, FT, GN])
        xe = sb("xe", [P, XSLOTS, D])
        xeT = sb("xeT", [P, UNITS, P])
        gelu_e = sb("gelu_e", [P, UNITS, FT, P])
        hid_e = sb("hid_e", [P, UNITS, FT, P])
        weighed = sb("weighed", [P, B, D])
        back = sb("back", [P, B, N], F32R)
        eo_full = sb("eo_full", [P, B, D])
        eo_hi = sb("eo_hi", [P, B, D], F32R)
        eo_lo = sb("eo_lo", [P, B, D], F32R)
        base_sb = sb("base_sb", [P, TILES, D])
        moeT = sb("moeT", [P, GROUPS, GN])
        y_sb = sb("y_sb", [P, TILES, D])

        def col(t, table, name):
            a, b = table[name]
            return t[:, a:b]

        def group(t, g):
            return t[:, g * GT:(g + 1) * GT, :]

        def tiled(p, width=P):
            return p.rearrange("p (t q) -> p t q", q=width)

        ident, flip = col(const_sb, CONST, "ident"), col(const_sb, CONST, "flip")
        blocks, heads = col(const_sb, CONST, "blocks"), col(const_sb, CONST, "heads")
        dec, epsdec = col(const_sb, CONST, "dec"), col(const_sb, CONST, "epsdec")
        eps_col = col(early_sb, EARLY, "eps")
        wmod_at = EARLY["wmod"][0]

        def modulation(j, b):
            return mod[:, j * B + b:j * B + b + 1]

        def gate_col(which, b):
            return gates[:, which, b:b + 1]

        psum = ctx.enter_context(nc.psum_tensor("psum", [P, 8 * GN], F32))

        def banks(i, n=1):
            return psum[:, i * GN:(i + n) * GN]

        q_ps, k_ps, v_ps = banks(0), banks(1), banks(2)
        kv_ps = (banks(3), banks(0))
        t_ps = (banks(4), banks(5))
        attT_ps = banks(5)
        route_ps = (banks(4), banks(6), banks(7), banks(4))
        o_ps = (banks(6, 2), banks(1, 2))
        y_ps = (banks(3), banks(0))
        mod_ps, ga_ps, warm_ps = banks(6), banks(7), banks(3)
        gb_ps, scoresT_ps = banks(5), banks(4)

        def norm_ps(n):
            return t_ps[n % 2] if n < GROUPS else route_ps[n - GROUPS]

        acc = (banks(0), banks(3), banks(5), banks(4))
        room = (banks(1), banks(2), banks(6), banks(7))
        hid_ps = room
        merge_ps = room[3]
        gu_ps, xeT_ps, eo_ps = room[0:2], room[2], room[3]

        x_in = [sem(f"x_in{g}") for g in range(GROUPS)]
        early_in, attn_in, const_in, bk_in = sem("early_in"), sem("attn_in"), sem("const_in"), sem("bk_in")
        bk_steps = sem("bk_steps")
        iota_in, shared_in = sem("iota_in"), sem("shared_in")
        w_in = [sem(f"w_in{n}") for n in range(WSLOTS)]
        rows_out, base_out = sem("rows_out"), sem("base_out")
        rows_in = [sem(f"rows_in{n}") for n in range(XSLOTS)]
        scattered = [sem(f"scattered{b}") for b in range(B)]
        base_in = [sem(f"base_in{b}") for b in range(B)]
        y_out = sem("y_out")

        ones_set = sem("ones_set")
        exp_c_done, silu_steps = sem("exp_c_done"), sem("silu_steps")
        mod_mm, ga_mm, mod_steps, gate_steps = sem("mod_mm"), sem("ga_mm"), sem("mod_steps"), sem("gate_steps")
        gadiag_done, gated_done = sem("gadiag_done"), sem("gated_done")
        gbdiag_done, gb_mm, gbrow_done = sem("gbdiag_done"), sem("gb_mm"), sem("gbrow_done")
        xg_done = sem("xg_done")
        stats_done, moments_done = sem("stats_done"), sem("moments_done")
        std_done, rstd_done = sem("std_done"), sem("rstd_done")
        xhat_dve, xhat_pool = sem("xhat_dve"), sem("xhat_pool")
        xT_mm, hT_done = sem("xT_mm"), sem("hT_done")
        q_mm, k_mm, v_mm, kv_mm = sem("q_mm"), sem("k_mm"), sem("v_mm"), sem("kv_mm")
        q_done, k_done, v_done = sem("q_done"), sem("k_done"), sem("v_done")
        ksum_done, kvfull_done, kv_done = sem("ksum_done"), sem("kvfull_done"), sem("kv_done")
        o_mm, den_done, rden_done, att_done = sem("o_mm"), sem("den_done"), sem("rden_done"), sem("att_done")
        attT_mm, attT_done = sem("attT_mm"), sem("attT_done")
        y_mm, x1_done = sem("y_mm"), sem("x1_done")
        logit_mm = sem("logit_mm")
        top_done, shift_done, expd_done = sem("top_done"), sem("shift_done"), sem("expd_done")
        total_done, rtotal_done, score_done = sem("total_done"), sem("rtotal_done"), sem("score_done")
        scoresT_mm = sem("scoresT_mm")
        max_done, place_done, strike_done, wheref_done = (sem("max_done"), sem("place_done"), sem("strike_done"),
                                                          sem("wheref_done"))
        lists_mm, merge_steps, flip_mm = sem("lists_mm"), sem("merge_steps"), sem("flip_mm")
        sg_mm, su_mm = sem("sg_mm"), sem("su_mm")
        sgelu_done, sup_done, shid_done, sdown_mm = sem("sgelu_done"), sem("sup_done"), sem("shid_done"), sem("sdown_mm")
        xeT_mm, xeT_done, gu_mm = sem("xeT_mm"), sem("xeT_done"), sem("gu_mm")
        gelu_done, hid_done, eo_mm = sem("gelu_done"), sem("hid_done"), sem("eo_mm")
        weighed_done, lo_done = sem("weighed_done"), sem("lo_done")
        hi_done, back_done, back_mm = sem("hi_done"), sem("back_done"), sem("back_mm")
        moe_act, moe_dve, moeT_mm, y_done = sem("moe_act"), sem("moe_dve"), sem("moeT_mm"), sem("y_done")

        MOD_COPIED, MOD_SCALES = 1, 3
        LISTED, MERGED = 1, 8
        BE = B * E

        def second(u):
            return u // B == 1

        def number(p):
            k, odd = p
            return k * 2 + odd

        def before(p):
            k, odd = p
            return (k, 0) if odd else (k - 1, 1)

        def after(p):
            k, odd = p
            return (k + 1, 0) if odd else (k, 1)

        def x_slot(p, u):
            return p[1] * UNITS + u

        def w_slot(p, u):
            return p[1] * 2 + u // B

        FIRST, LAST = (0, 0), (PAIRS // 2 - 1, 1)

        def same(p, q):
            return isinstance(p[0], int) and p == q

        def all_steps(engine, step):
            for u in range(UNITS):
                step(FIRST, u)
            step(after(FIRST), 0)
            with engine.Fori(0, PAIRS // 2 - 1) as k:
                for u in range(1, UNITS):
                    step((k, 1), u)
                for u in range(UNITS):
                    step((k + 1, 0), u)
                step((k + 1, 1), 0)
            for u in range(1, UNITS):
                step(LAST, u)

        block = ctx.enter_context(nc.Block())

        @block.sync
        def _(sp):
            sp.dma_start(group(x_sb, 0), group(x_v, 0)).then_inc(x_in[0], 16)
            sp.dma_start(early_sb[:, :], early).then_inc(early_in, 16)
            sp.dma_start(group(x_sb, 1), group(x_v, 1)).then_inc(x_in[1], 16)
            sp.dma_start(const_sb[:, :], const).then_inc(const_in, 16)
            sp.dma_start(attn_sb[:, :], attn).then_inc(attn_in, 16)
            sp.dma_start(bk_sb[:, :], bk_row).then_inc(bk_in, 16)
            for g in range(2, GROUPS):
                sp.dma_start(group(x_sb, g), group(x_v, g)).then_inc(x_in[g], 16)
            sp.dma_start(wshared[:, :], wexp[E, :, :]).then_inc(shared_in, 16)
            sp.dma_start(iota_sb[:, :], iota).then_inc(iota_in, 16)
            for n in range(WSLOTS):
                sp.dma_start(wring[:, n, :], wexp[n, :, :]).then_inc(w_in[n], 16)
            for g in range(GROUPS):
                rows = slice((g % GPB) * GN, (g % GPB + 1) * GN)
                sp.wait_ge(x1_done, g + 1)
                sp.dma_start(base_rows[g // GPB][rows, :].rearrange("(t p) d -> p t d", p=P), group(xg, g)).then_inc(base_out, 16)
                sp.wait_ge(xhat_dve, (GROUPS + g + 1) * GT // 2)
                sp.wait_ge(xhat_pool, (GROUPS + g + 1) * GT // 2)
                sp.dma_start(xhat_rows[g // GPB][rows, :].rearrange("(t p) d -> p t d", p=P), group(xhat, g)).then_inc(rows_out, 16)
            with sp.Fori(1, PAIRS // 2) as k:
                for n in range(WSLOTS):
                    sp.wait_ge(eo_mm, (k - 1) * 2 * UNITS + B * (n + 1))
                    sp.dma_start(wring[:, n, :], wexp[bass.ds(k * WSLOTS + n, 1), :, :].rearrange("a p n -> p (a n)")).then_inc(w_in[n], 16)
            for b in range(B):
                sp.wait_ge(scattered[b], 16 * (PAIRS))
                sp.dma_start(base_sb[:, b * TPB:(b + 1) * TPB, :], base_rows[b].rearrange("(t p) d -> p t d", p=P))\
                    .then_inc(base_in[b], 16)
            for g in range(GROUPS):
                sp.wait_ge(y_done, g + 1)
                sp.dma_start(group(out_v, g), group(y_sb, g)).then_inc(y_out, 16)
            sp.wait_ge(y_out, 16 * GROUPS)

        @block.gpsimd
        def _(pool):
            def normalise(n, src):
                g = n % GROUPS
                pool.wait_ge(rstd_done, 2 * n + 2)
                if n >= GROUPS:
                    pool.wait_ge(xT_mm, g + 1)
                for t in range(GT // 2):
                    m = n * GT + t
                    pool.tensor_scalar(xhat[:, g * GT + t, :], src[:, g * GT + t, :], minus_mean[:, m:m + 1], rstd[:, m:m + 1],
                                       op0=ALU.add, op1=ALU.mult).then_inc(xhat_pool, 1)

            for n in range(GROUPS):
                normalise(n, x_sb)
            pool.wait_ge(gated_done, 2)
            for g in range(GROUPS):
                pool.tensor_tensor(group(xg, g), group(x_sb, g),
                                   bo_gated[:, g // GPB:g // GPB + 1, :].to_broadcast([P, GT, D]),
                                   op=ALU.add).then_inc(xg_done, 1)
            pool.wait_ge(gate_steps, 4)
            for b in range(B):
                pool.tensor_scalar(gb_diag[:, b, :], ident, gate_col(1, b), 0.0, op0=ALU.mult, op1=ALU.add).then_inc(gbdiag_done, 1)
            for n in range(GROUPS, 2 * GROUPS):
                normalise(n, xg)
            for c in range(GROUPS):
                for f in range(FT):
                    n = c * FT + f + 1
                    pool.wait_ge(sgelu_done, n)
                    pool.wait_ge(sup_done, n)
                    if c >= 2:
                        pool.wait_ge(sdown_mm, c - 1)
                    pool.tensor_tensor(hid_s[:, c % 2, f, :], gelu_s[:, c % 2, f, :], up_s[:, c % 2, f, :],
                                       op=ALU.mult).then_inc(shid_done, 1)

            def expert_batch(n):
                return n // B, n % B

            def gather(n):
                e, b = expert_batch(n)
                if n >= XSLOTS:
                    pool.wait_ge(xeT_mm, n - XSLOTS + 1)
                pool.indirect_dma_start(
                    out=xe[:, n % XSLOTS, :], out_offset=None, in_=xhat_rows[b],
                    in_offset=bass.IndirectOffsetOnAxis(ap=chosen_row[:, e, b:b + 1], axis=0)).then_inc(rows_in[n % XSLOTS], 16)

            def scatter(n):
                e, b = expert_batch(n)
                if n >= UNITS:
                    pool.wait_ge(scattered[b], 16 * (n // UNITS))
                pool.wait_ge(weighed_done, n // UNITS * B + b + 1)
                pool.indirect_dma_start(
                    out=base_rows[b], out_offset=bass.IndirectOffsetOnAxis(ap=chosen_row[:, e, b:b + 1], axis=0),
                    in_=weighed[:, b, :], in_offset=None, compute_op=ALU.add).then_inc(scattered[b], 16)

            pool.wait_ge(rows_out, 16 * GROUPS)
            pool.wait_ge(base_out, 16 * GROUPS)
            pool.wait_ge(merge_steps, MERGED)
            for n in range(-AHEAD, B * E):
                if n + AHEAD < B * E:
                    gather(n + AHEAD)
                if n >= 1 and not second((n - 1) % UNITS):
                    scatter(n - 1)

        @block.scalar
        def _(act):
            act.wait_ge(early_in, 16)
            act.activation(exp_c[:, :], col(early_sb, EARLY, "c"), ACT.Exp, scale=-1.0).then_inc(exp_c_done, 1)

            def norm_std(n):
                act.wait_ge(moments_done, (n + 1) * GT)
                act.activation(std[:, n * GT:(n + 1) * GT], moments[:, n * GT:(n + 1) * GT, 1], ACT.Sqrt,
                               bias=eps_col).then_inc(std_done, 1)

            def modulated(n, scale, shift):
                g = n % GROUPS
                act.wait_ge(xT_mm, n + 1)
                act.activation(group(hT, g), tiled(norm_ps(n)), ACT.Identity, scale=scale[:, g // GPB:g // GPB + 1],
                               bias=modulation(shift, g // GPB)).then_inc(hT_done, 1)

            def modulated_a(g):
                if g == 0:
                    act.wait_ge(mod_steps, MOD_SCALES)
                modulated(g, scale_a, MOD_SA)

            def query(g):
                act.wait_ge(q_mm, g + 1)
                act.activation(group(qT, g), tiled(q_ps), ACT.Relu, bias=col(early_sb, EARLY, "bq")).then_inc(q_done, 1)

            def key(g):
                act.wait_ge(k_mm, g + 1)
                if g >= 2:
                    act.wait_ge(kv_mm, g - 1)
                act.activation(k_sb[:, g % 2, :, :], tiled(k_ps), ACT.Relu).then_inc(k_done, 1)

            norm_std(0)
            modulated_a(0)
            norm_std(1)
            norm_std(2)
            modulated_a(1)
            norm_std(3)
            for g in range(GROUPS):
                query(g)
                key(g)
                if g + 2 < GROUPS:
                    modulated_a(g + 2)

            def attention_out(g):
                act.wait_ge(attT_mm, g + 1)
                if g >= 2:
                    act.wait_ge(y_mm, g - 1)
                act.activation(attT[:, g % 2, :, :], tiled(attT_ps), ACT.Copy).then_inc(attT_done, 1)

            def modulated_b(g):
                modulated(GROUPS + g, scale_b, MOD_SB)

            attention_out(0)
            attention_out(1)
            norm_std(GROUPS)
            modulated_b(0)
            attention_out(2)
            norm_std(GROUPS + 1)
            attention_out(3)
            norm_std(GROUPS + 2)
            modulated_b(1)
            norm_std(GROUPS + 3)
            modulated_b(2)
            modulated_b(3)
            for b in range(B):
                act.wait_ge(shift_done, (b + 1) * GPB)
                at = slice(b * TPB, (b + 1) * TPB)
                act.activation(expd[:, at, :], shifted[:, at, :], ACT.Exp).then_inc(expd_done, 1)
            act.wait_ge(gb_mm, 1)
            act.activation(gb_row[:, :, :], tiled(gb_ps[:, 0:B * D]), ACT.Copy).then_inc(gbrow_done, 1)
            for c in range(GROUPS):
                for f in range(FT):
                    n = c * FT + f + 1
                    act.wait_ge(sg_mm, n)
                    if c >= 2:
                        act.wait_ge(shid_done, n - 2 * FT)
                    act.activation(gelu_s[:, c % 2, f, :], hid_ps[f], ACT.Gelu).then_inc(sgelu_done, 1)
                    act.wait_ge(su_mm, n)
                    act.activation(up_s[:, c % 2, f, :], hid_ps[FT + f], ACT.Copy).then_inc(sup_done, 1)

            def evacuate_x(p, u):
                b = u % B
                act.wait_ge(xeT_mm, number(p) * UNITS + u + 1)
                act.activation(xeT[:, u, :], xeT_ps[:, u * P:(u + 1) * P], ACT.Identity,
                               scale=scale_b[:, b:b + 1], bias=modulation(MOD_SB, b)).then_inc(xeT_done, 1)

            def gelu(p, u):
                act.wait_ge(gu_mm, number(p) * UNITS + u + 1)
                act.activation(gelu_e[:, u, :, :], tiled(gu_ps[u % 2][:, 0:F]), ACT.Gelu).then_inc(gelu_done, 1)

            def high_part(p, u):
                b = u % B
                act.wait_ge(eo_mm, number(p) * UNITS + u + 1)
                if not same(p, FIRST):
                    act.wait_ge(back_mm, number(before(p)) * B + b + 1)
                act.activation(eo_hi[:, b, :], eo_ps[:, 0:D], ACT.Copy,
                               scale=chosen_w[:, bass.ds(number(p) * 2 + 1, 1), b]).then_inc(hi_done, 1)
                act.activation(eo_full[:, b, :], eo_ps[:, 0:D], ACT.Copy,
                               scale=chosen_w[:, bass.ds(number(p) * 2 + 1, 1), b]).then_inc(hi_done, 1)

            def step(p, u):
                if u + 1 < UNITS:
                    evacuate_x(p, u + 1)
                elif not same(p, LAST):
                    evacuate_x(after(p), 0)
                gelu(p, u)
                if u == 3:
                    high_part(p, 2)
                elif u == 0 and not same(p, FIRST):
                    high_part(before(p), 3)

            def gate_moe(g):
                act.wait_ge(back_mm, B * (PAIRS - 1) + g // GPB + 1)
                act.activation(moeT[:, g, :], acc[g], ACT.Copy, scale=gate_col(1, g // GPB)).then_inc(moe_act, 1)

            act.wait_ge(merge_steps, MERGED)
            evacuate_x(FIRST, 0)
            all_steps(act, step)
            high_part(LAST, UNITS - 1)
            for g in range(GROUPS - 1):
                gate_moe(g)

        @block.vector
        def _(dve):
            dve.memset(ones[:, :], 1.0).then_inc(ones_set, 1)
            dve.wait_ge(ones_set, 1)
            dve.tensor_copy(ones_two[:, :], ones[0:2, 0:P]).then_inc(ones_set, 1)

            def norm_stats(n, src):
                g = n % GROUPS
                for t in range(GT):
                    dve.bn_stats(stats[:, n * GT + t, :], src[:, g * GT + t, :]).then_inc(stats_done, 1)
                for t in range(GT):
                    dve.wait_ge(stats_done, n * GT + t + 1)
                    dve.bn_aggr(moments[:, n * GT + t, :], stats[:, n * GT + t, :]).then_inc(moments_done, 1)

            def normalise(n, src):
                g = n % GROUPS
                at = slice(n * GT, (n + 1) * GT)
                dve.wait_ge(moments_done, (n + 1) * GT)
                dve.tensor_scalar_mul(minus_mean[:, at], moments[:, at, 0], -1.0).then_inc(rstd_done, 1)
                dve.wait_ge(std_done, n + 1)
                dve.reciprocal(rstd[:, at], std[:, at]).then_inc(rstd_done, 1)
                dve.wait_ge(rstd_done, 2 * n + 2)
                if n >= GROUPS:
                    dve.wait_ge(xT_mm, g + 1)
                for t in range(GT // 2, GT):
                    m = n * GT + t
                    dve.tensor_scalar(xhat[:, g * GT + t, :], src[:, g * GT + t, :], minus_mean[:, m:m + 1], rstd[:, m:m + 1],
                                      op0=ALU.add, op1=ALU.mult).then_inc(xhat_dve, 1)

            dve.wait_ge(x_in[0], 16)
            norm_stats(0, x_sb)
            dve.wait_ge(exp_c_done, 1)
            dve.tensor_scalar_add(exp_c1[:, :], exp_c[:, :], 1.0).then_inc(silu_steps, 1)
            dve.wait_ge(silu_steps, 1)
            dve.reciprocal(sig_c[:, :], exp_c1[:, :]).then_inc(silu_steps, 1)
            dve.wait_ge(silu_steps, 2)
            dve.tensor_tensor(silu_c[:, :], col(early_sb, EARLY, "c"), sig_c[:, :], op=ALU.mult).then_inc(silu_steps, 1)
            normalise(0, x_sb)
            dve.wait_ge(x_in[1], 16)
            norm_stats(1, x_sb)
            dve.wait_ge(mod_mm, 1)
            dve.tensor_copy(mod[:, :], mod_ps[:, 0:6 * B]).then_inc(mod_steps, 1)
            dve.wait_ge(mod_steps, MOD_COPIED)
            dve.tensor_scalar_add(scale_a[:, :], mod[:, MOD_CA * B:(MOD_CA + 1) * B], 1.0).then_inc(mod_steps, 1)
            dve.tensor_scalar_add(scale_b[:, :], mod[:, MOD_CB * B:(MOD_CB + 1) * B], 1.0).then_inc(mod_steps, 1)
            normalise(1, x_sb)
            dve.wait_ge(bk_in, 16)
            dve.tensor_copy(bk_high[:, :], bk_sb[:, 0:D]).then_inc(bk_steps, 1)
            dve.wait_ge(bk_steps, 1)
            dve.tensor_scalar_mul(bk_rest[:, :], bk_high[:, :].bitcast(F32), bk_sb[:, D:D + 1]).then_inc(bk_steps, 1)
            dve.wait_ge(bk_steps, 2)
            dve.scalar_tensor_tensor(bk_parts[:, :], bk_sb[:, 0:D], bk_sb[:, D + 1:D + 2], bk_rest[:, :],
                                     op0=ALU.mult, op1=ALU.add).then_inc(bk_steps, 1)
            dve.wait_ge(x_in[2], 16)
            norm_stats(2, x_sb)
            raw = mod[:, :].rearrange("p (j b) -> p j b", b=B)[:, MOD_GA:MOD_GB + 1:MOD_GB - MOD_GA, :]
            dve.tensor_scalar(gate_sign[:, :, :], raw, 0.0, 2.0, op0=ALU.is_ge, op1=ALU.mult).then_inc(gate_steps, 1)
            dve.tensor_scalar(gate_turned[:, :, :], raw, -1.0, 0.25, op0=ALU.mult, op1=ALU.max).then_inc(gate_steps, 1)
            dve.wait_ge(gate_steps, 2)
            dve.scalar_tensor_tensor(gate_size[:, :, :], raw, 0.25, gate_turned[:, :, :], op0=ALU.max, op1=ALU.max)\
                .then_inc(gate_steps, 1)
            dve.wait_ge(gate_steps, 3)
            dve.scalar_tensor_tensor(gates[:, :, :], gate_sign[:, :, :], -1.0, gate_size[:, :, :], op0=ALU.add, op1=ALU.mult)\
                .then_inc(gate_steps, 1)
            dve.wait_ge(gate_steps, 4)
            dve.wait_ge(const_in, 16)
            for b in range(B):
                dve.tensor_scalar_mul(ga_diag[:, b, :], ident, gate_col(0, b)).then_inc(gadiag_done, 1)
            normalise(2, x_sb)
            dve.wait_ge(x_in[3], 16)
            norm_stats(3, x_sb)
            normalise(3, x_sb)
            dve.wait_ge(ga_mm, 1)
            dve.wait_ge(attn_in, 16)
            for name, gated in (("wo", wo_gated), ("bo", bo_gated)):
                dve.tensor_tensor(gated[:, :, :], tiled(ga_ps[:, 0:B * D]),
                                  col(attn_sb, ATTN, name).unsqueeze(1).to_broadcast([P, B, D]),
                                  op=ALU.mult).then_inc(gated_done, 1)

            def heads_of(b):
                dve.wait_ge(kv_mm, (b + 1) * GPB)
                dve.tensor_copy(ksum[:, b:b + 1], kv_ps[b][:, D:D + 1]).then_inc(ksum_done, 1)
                dve.wait_ge(ksum_done, b + 1)
                dve.scalar_tensor_tensor(kv_full[:, b, :], col(attn_sb, ATTN, "bv"), ksum[:, b:b + 1],
                                         kv_ps[b][:, 0:D], op0=ALU.mult, op1=ALU.add).then_inc(kvfull_done, 1)
                dve.tensor_scalar_mul(kv_heads[:, b, D:D + H], heads, ksum[:, b:b + 1]).then_inc(kv_done, 1)
                dve.wait_ge(kvfull_done, b + 1)
                dve.tensor_tensor(kv_heads[:, b, 0:D], kv_full[:, b, :], blocks, op=ALU.mult).then_inc(kv_done, 1)

            for g in range(GROUPS):
                if g >= 2:
                    dve.wait_ge(kv_mm, g - 1)
                dec_g = dec[:, (g % GPB) * GT:(g % GPB + 1) * GT].unsqueeze(2)
                dve.tensor_copy(v_sb[:, g % 2, :, D:D + 1], dec_g).then_inc(v_done, 1)
                dve.wait_ge(v_mm, g + 1)
                dve.tensor_tensor(v_sb[:, g % 2, :, 0:D], tiled(v_ps), dec_g.to_broadcast([P, GT, D]),
                                  op=ALU.mult).then_inc(v_done, 1)
                if g == GPB:
                    heads_of(0)

            def divide(g):
                s = g % 2
                dve.wait_ge(o_mm, g + 1)
                if g >= 2:
                    dve.wait_ge(attT_mm, g - 1)
                eps_g = epsdec[:, (g % GPB) * GT:(g % GPB + 1) * GT]
                o = tiled(o_ps[s], 256)
                dve.tensor_tensor(den[:, s, :, :], o[:, :, D:D + H], eps_g.unsqueeze(2).to_broadcast([P, GT, H]),
                                  op=ALU.add).then_inc(den_done, 1)
                dve.wait_ge(den_done, g + 1)
                dve.reciprocal(rden[:, s, :, :], den[:, s, :, :]).then_inc(rden_done, 1)
                dve.wait_ge(rden_done, g + 1)
                dve.tensor_tensor(att[:, s, :, :].rearrange("p t (h k) -> p t h k", h=H),
                                  o[:, :, 0:D].rearrange("p t (h k) -> p t h k", h=H),
                                  rden[:, s, :, :].unsqueeze(3).to_broadcast([P, GT, H, D // H]),
                                  op=ALU.mult).then_inc(att_done, 1)

            def residual(g):
                dve.wait_ge(y_mm, g + 1)
                dve.wait_ge(xg_done, g + 1)
                dve.tensor_tensor(group(xg, g), group(xg, g), tiled(y_ps[g % 2]), op=ALU.add).then_inc(x1_done, 1)
                dve.wait_ge(x1_done, g + 1)

            def soften_in(g):
                at = slice(g * GT, (g + 1) * GT)
                logits = tiled(route_ps[g][:, 0:GT * E], E)
                dve.wait_ge(logit_mm, g + 1)
                dve.tensor_reduce(top[:, at], logits, axis=AX_X, op=ALU.max).then_inc(top_done, 1)
                dve.wait_ge(top_done, g + 1)
                dve.tensor_tensor(shifted[:, at, :], logits, top[:, at].unsqueeze(2).to_broadcast([P, GT, E]),
                                  op=ALU.subtract).then_inc(shift_done, 1)

            def soften_out():
                for b in range(B):
                    at = slice(b * TPB, (b + 1) * TPB)
                    dve.wait_ge(expd_done, b + 1)
                    dve.tensor_reduce(total[:, at], expd[:, at, :], axis=AX_X, op=ALU.add).then_inc(total_done, 1)
                dve.wait_ge(total_done, B)
                dve.reciprocal(rtotal[:, :], total[:, :]).then_inc(rtotal_done, 1)
                dve.wait_ge(rtotal_done, 1)
                for b in range(B):
                    at = slice(b * TPB, (b + 1) * TPB)
                    dve.tensor_tensor(scores[:, :, :, b, :], expd[:, at, :].rearrange("p (h q) e -> p q h e", h=2),
                                      rtotal[:, at].rearrange("p (h q) -> p q h", h=2).unsqueeze(3).to_broadcast([P, QUARTERS, 2, E]),
                                      op=ALU.mult).then_inc(score_done, 1)

            divide(0)
            divide(1)
            heads_of(1)
            for g in range(GROUPS):
                residual(g)
                norm_stats(GROUPS + g, xg)
                if g < GPB:
                    divide(g + 2)
                    normalise(GROUPS + g, xg)
            normalise(GROUPS + 2, xg)
            soften_in(0)
            normalise(GROUPS + 3, xg)
            soften_in(1)
            soften_in(2)
            soften_in(3)
            soften_out()

            dve.wait_ge(scoresT_mm, 1)
            for r in range(ROUNDS):
                at = slice(8 * r, 8 * r + 8)
                now, then = work[:, r % 2, :] if r else scoresT_ps[0:ROWS, :], work[:, (r + 1) % 2, :]
                if r:
                    dve.wait_ge(strike_done, r)
                dve.max(best[:, at], now).then_inc(max_done, 1)
                dve.wait_ge(max_done, r + 1)
                if r < ROUNDS - 1:
                    if r:
                        dve.wait_ge(place_done, r)
                    dve.match_replace(then, best[:, at], now, -1.0).then_inc(strike_done, 1)
                dve.max_index(where[:, at], best[:, at], now).then_inc(place_done, 1)
            dve.wait_ge(place_done, ROUNDS)
            dve.tensor_copy(wheref[:, :], where[:, :]).then_inc(wheref_done, 1)
            dve.wait_ge(lists_mm, 1)
            dve.tensor_copy(lists[:, :, :, :], merge_ps[:, 0:4 * BE].rearrange("p (k h r) -> p k h r", k=2, h=2))\
                .then_inc(merge_steps, 1)
            dve.wait_ge(flip_mm, 1)
            flipped = merge_ps[:, 4 * BE:6 * BE].rearrange("p (k r) -> p k r", k=2)

            def by_batch(a):
                return a.rearrange("p (b e) -> p b e", b=B)

            dve.tensor_scalar_add(second_place[:, :], flipped[:, 1, :], float(HALF)).then_inc(merge_steps, 1)
            dve.tensor_tensor(first_wins[:, :], lists[:, 0, 0, :], flipped[:, 0, :], op=ALU.is_ge).then_inc(merge_steps, 1)
            dve.wait_ge(merge_steps, LISTED + 1)
            dve.tensor_tensor(place_gap[:, :], lists[:, 1, 0, :], second_place[:, :], op=ALU.subtract).then_inc(merge_steps, 1)
            dve.tensor_tensor(chosen_w[:, :, :].rearrange("p e b -> p b e"), by_batch(lists[:, 0, 0, :]),
                              by_batch(flipped[:, 0, :]), op=ALU.max).then_inc(merge_steps, 1)
            dve.wait_ge(merge_steps, LISTED + 3)
            dve.tensor_tensor(place_add[:, :], place_gap[:, :], first_wins[:, :], op=ALU.mult).then_inc(merge_steps, 1)
            dve.wait_ge(merge_steps, LISTED + 5)
            for chosen in (chosen_row, chosen_at):
                dve.tensor_tensor(chosen[:, :, :].rearrange("p e b -> p b e"), by_batch(second_place[:, :]),
                                  by_batch(place_add[:, :]), op=ALU.add).then_inc(merge_steps, 1)

            def way_back(p, b):
                if not same(p, FIRST):
                    dve.wait_ge(back_mm, number(before(p)) * B + b + 1)
                dve.tensor_scalar(back[:, b, :], iota_sb[:, :], chosen_at[:, bass.ds(number(p) * 2 + 1, 1), b], None,
                                  op0=ALU.is_equal).then_inc(back_done, 1)

            def hidden(p, u):
                dve.wait_ge(gelu_done, number(p) * UNITS + u + 1)
                dve.tensor_tensor(hid_e[:, u, :, :], gelu_e[:, u, :, :], tiled(gu_ps[u % 2][:, F:2 * F]),
                                  op=ALU.mult).then_inc(hid_done, 1)

            def take_out(p, u):
                b = u % B
                w = chosen_w[:, bass.ds(number(p) * 2 + u // B, 1), b]
                if second(u):
                    dve.wait_ge(hi_done, (number(p) * B + b + 1) * 2)
                    dve.tensor_tensor(eo_lo[:, b, :], eo_full[:, b, :], eo_hi[:, b, :].bitcast(F32),
                                      op=ALU.subtract).then_inc(lo_done, 1)
                else:
                    if not same(p, FIRST):
                        dve.wait_ge(scattered[b], number(p) * 16)
                    dve.wait_ge(eo_mm, number(p) * UNITS + u + 1)
                    dve.scalar_tensor_tensor(weighed[:, b, :], eo_ps[:, 0:D], w, gb_row[:, b, :],
                                             op0=ALU.mult, op1=ALU.mult).then_inc(weighed_done, 1)

            def step(p, u):
                hidden(p, u)
                if u:
                    take_out(p, u - 1)
                elif not same(p, FIRST):
                    take_out(before(p), UNITS - 1)
                if second(u):
                    way_back(p, u % B)

            dve.wait_ge(iota_in, 16)
            dve.wait_ge(gbrow_done, 1)
            dve.wait_ge(merge_steps, MERGED)
            all_steps(dve, step)
            take_out(LAST, UNITS - 1)
            dve.wait_ge(back_mm, B * (PAIRS))
            dve.tensor_scalar_mul(moeT[:, GROUPS - 1, :], acc[GROUPS - 1], gate_col(1, B - 1)).then_inc(moe_dve, 1)
            for g in range(GROUPS):
                if g % GPB == 0:
                    dve.wait_ge(base_in[g // GPB], 16)
                dve.wait_ge(moeT_mm, g + 1)
                dve.tensor_tensor(group(y_sb, g), group(base_sb, g), tiled(room[g]), op=ALU.add).then_inc(y_done, 1)

        @block.tensor
        def _(pe):
            pe.wait_ge(ones_set, 1)
            for _ in range(WARM):
                pe.matmul(warm_ps, ones[:, 0:P], ones[:, :], start=True, stop=True)
            pe.wait_ge(silu_steps, 3)
            pe.wait_ge(early_in, 16)
            for j in range(6):
                last = pe.matmul(mod_ps[:, j * B:(j + 1) * B], early_sb[:, wmod_at + j * D:wmod_at + (j + 1) * D],
                                 silu_c[:, :], start=True, stop=True)
            last.then_inc(mod_mm, 1)

            def transposes(n):
                g = n % GROUPS
                pe.wait_ge(xhat_pool, (n + 1) * GT // 2)
                for t in range(GT):
                    if t == GT // 2:
                        pe.wait_ge(xhat_dve, (n + 1) * GT // 2)
                    last = pe.transpose(norm_ps(n)[:, t * P:(t + 1) * P], xhat[:, g * GT + t, :], ident)
                last.then_inc(xT_mm, 1)

            def query(g):
                pe.wait_ge(hT_done, g + 1)
                if g:
                    pe.wait_ge(q_done, g)
                pe.matmul(tiled(q_ps), col(attn_sb, ATTN, "wq"), group(hT, g), start=True, stop=True).then_inc(q_mm, 1)

            def key(g):
                if g:
                    pe.wait_ge(k_done, g)
                pe.matmul(tiled(k_ps), ones_two[:, :], bk_parts[:, :].unsqueeze(1).to_broadcast([2, GT, D]), start=True, stop=False)
                for t in range(GT):
                    last = pe.matmul(k_ps[:, t * D:(t + 1) * D], hT[:, g * GT + t, :], col(attn_sb, ATTN, "wk"),
                                     start=False, stop=t == GT - 1)
                last.then_inc(k_mm, 1)

            def value(g):
                if g:
                    pe.wait_ge(v_done, 2 * g)
                for t in range(GT):
                    last = pe.matmul(v_ps[:, t * D:(t + 1) * D], hT[:, g * GT + t, :], col(attn_sb, ATTN, "wv"),
                                     start=True, stop=True)
                last.then_inc(v_mm, 1)

            def sum_kv(g):
                pe.wait_ge(k_done, g + 1)
                pe.wait_ge(v_done, 2 * g + 2)
                if g == GPB:
                    pe.wait_ge(q_done, GROUPS)
                for t in range(GT):
                    n = (g % GPB) * GT + t
                    last = pe.matmul(kv_ps[g // GPB][:, 0:D + 1], k_sb[:, g % 2, t, :], v_sb[:, g % 2, t, :],
                                     start=n == 0, stop=n == TPB - 1)
                last.then_inc(kv_mm, 1)

            pe.wait_ge(const_in, 16)
            transposes(0)
            pe.wait_ge(attn_in, 16)
            query(0)
            transposes(1)
            pe.wait_ge(bk_steps, 3)
            key(0)
            pe.wait_ge(hT_done, 1)
            transposes(2)
            value(0)
            pe.wait_ge(gadiag_done, B)
            pe.matmul(ga_ps[:, 0:B * D], ones[:, 0:P], ga_diag[:, :, :].rearrange("p b d -> p (b d)"), start=True, stop=True)\
                .then_inc(ga_mm, 1)
            for g in range(1, GROUPS):
                query(g)
                key(g)
                if g == 1:
                    pe.wait_ge(hT_done, 2)
                    transposes(3)
                value(g)
                if g < GROUPS - 1:
                    sum_kv(g - 1)

            def attend(g):
                b = g // GPB
                if g % GPB == 0:
                    pe.wait_ge(kv_done, 2 * b + 2)
                if g == 0:
                    pe.wait_ge(gated_done, 2)
                if g == 1:
                    pe.wait_ge(k_done, GROUPS)
                    pe.wait_ge(v_done, 2 * GROUPS)
                if g >= 2:
                    pe.wait_ge(att_done, g - 1)
                for t in range(GT):
                    last = pe.matmul(o_ps[g % 2][:, t * 256:t * 256 + D + H], qT[:, g * GT + t, :], kv_heads[:, b, :],
                                     start=True, stop=True)
                last.then_inc(o_mm, 1)

            def turn_attention(g):
                pe.wait_ge(att_done, g + 1)
                pe.wait_ge(hT_done, GROUPS)
                if g:
                    pe.wait_ge(attT_done, g)
                for t in range(GT):
                    last = pe.transpose(attT_ps[:, t * P:(t + 1) * P], att[:, g % 2, t, :], ident)
                last.then_inc(attT_mm, 1)

            def project(g):
                pe.wait_ge(attT_done, g + 1)
                if g < 2:
                    pe.wait_ge(kvfull_done, g + 1)
                else:
                    pe.wait_ge(x1_done, g - 1)
                for t in range(GT):
                    last = pe.matmul(y_ps[g % 2][:, t * D:(t + 1) * D], attT[:, g % 2, t, :], wo_gated[:, g // GPB, :],
                                     start=True, stop=True)
                last.then_inc(y_mm, 1)

            def route(g):
                pe.wait_ge(hT_done, GROUPS + g + 1)
                for t in range(GT):
                    last = pe.matmul(route_ps[g][:, t * E:(t + 1) * E], hT[:, g * GT + t, :], col(attn_sb, ATTN, "gate"),
                                     start=True, stop=True)
                last.then_inc(logit_mm, 1)

            def shared_gate(c, f):
                if c:
                    pe.wait_ge(sgelu_done, (c - 1) * FT + f + 1)
                pe.matmul(tiled(hid_ps[f]), wshared[:, f * P:(f + 1) * P], group(hT, c), start=True, stop=True).then_inc(sg_mm, 1)

            def shared_up(c, f):
                if c:
                    pe.wait_ge(sup_done, (c - 1) * FT + f + 1)
                pe.matmul(tiled(hid_ps[FT + f]), wshared[:, (FT + f) * P:(FT + f + 1) * P], group(hT, c),
                          start=True, stop=True).then_inc(su_mm, 1)

            def shared_down(c):
                pe.wait_ge(shid_done, (c + 1) * FT)
                for f in range(FT):
                    last = pe.matmul(acc[c], wshared[:, (2 * FT + f) * P:(2 * FT + f + 1) * P], hid_s[:, c % 2, f, :],
                                     start=f == 0, stop=False, skip_group_check=True)
                last.then_inc(sdown_mm, 1)

            attend(0)
            sum_kv(GROUPS - 2)
            attend(1)
            turn_attention(0)
            sum_kv(GROUPS - 1)
            project(0)
            turn_attention(1)
            attend(2)
            project(1)
            transposes(GROUPS)
            attend(3)
            turn_attention(2)
            project(2)
            turn_attention(3)
            route(0)
            project(3)
            pe.wait_ge(att_done, GROUPS)
            transposes(GROUPS + 1)
            route(1)
            pe.wait_ge(shared_in, 16)
            shared_gate(0, 0)
            transposes(GROUPS + 2)
            pe.wait_ge(shift_done, 1)
            transposes(GROUPS + 3)
            route(2)
            route(3)
            shared_gate(0, 1)
            pe.wait_ge(score_done, B)
            for q in range(QUARTERS):
                last = pe.transpose(scoresT_ps[0:ROWS, q * P:(q + 1) * P], scores[:, q, :, :, :].rearrange("p h b e -> p (h b e)"), ident)
            last.then_inc(scoresT_mm, 1)

            pe.wait_ge(gbdiag_done, B)
            pe.wait_ge(attT_done, GROUPS)
            pe.matmul(gb_ps[:, 0:B * D], ones[:, 0:P], gb_diag[:, :, :].rearrange("p b d -> p (b d)"), start=True, stop=True)\
                .then_inc(gb_mm, 1)
            pe.wait_ge(shift_done, GROUPS - 1)
            shared_up(0, 0)
            shared_up(0, 1)
            for c in range(1, GROUPS):
                if c == 2:
                    pe.wait_ge(max_done, LATE_ROUND)
                for f in range(FT):
                    shared_gate(c, f)
                    shared_up(c, f)
                if c == 1:
                    pe.wait_ge(x1_done, GROUPS)
                if c < GROUPS - 1:
                    shared_down(c - 1)

            pe.wait_ge(sup_done, GROUPS * FT)
            pe.wait_ge(wheref_done, 1)
            pe.transpose(merge_ps[:, 0:ROWS], best[:, :], ident[0:ROWS, 0:ROWS])
            pe.transpose(merge_ps[:, ROWS:2 * ROWS], wheref[:, :], ident[0:ROWS, 0:ROWS]).then_inc(lists_mm, 1)
            pe.wait_ge(merge_steps, LISTED)
            for k in range(2):
                last = pe.matmul(merge_ps[:, (4 + k) * BE:(5 + k) * BE], flip, lists[:, k, 1, :], start=True, stop=True)
            last.then_inc(flip_mm, 1)
            pe.wait_ge(gbrow_done, 1)
            shared_down(GROUPS - 2)
            shared_down(GROUPS - 1)

            def turn(p, u, first=False):
                pe.wait_ge(rows_in[x_slot(p, u)], (p[0] + 1) * 16)
                if not first:
                    pe.wait_ge(xeT_done, number(p) * UNITS + u)
                pe.transpose(xeT_ps[:, u * P:(u + 1) * P], xe[:, x_slot(p, u), :], ident).then_inc(xeT_mm, 1)

            def gate_up(p, u):
                if u % B == 0:
                    pe.wait_ge(w_in[w_slot(p, u)], (p[0] + 1) * 16)
                pe.wait_ge(xeT_done, number(p) * UNITS + u + 1)
                for j in range(2 * FT):
                    last = pe.matmul(gu_ps[u % 2][:, j * P:(j + 1) * P], wring[:, w_slot(p, u), j * P:(j + 1) * P], xeT[:, u, :],
                                     start=True, stop=True)
                last.then_inc(gu_mm, 1)

            def down(p, u):
                pe.wait_ge(hid_done, number(p) * UNITS + u + 1)
                if u == 0:
                    if not same(p, FIRST):
                        pe.wait_ge(hi_done, number(p) * B * 2)
                elif second(u - 1):
                    pe.wait_ge(hi_done, (number(p) * B + u - B) * 2)
                else:
                    pe.wait_ge(weighed_done, number(p) * B + u)
                for f in range(FT):
                    last = pe.matmul(eo_ps[:, 0:D], hid_e[:, u, f, :],
                                     wring[:, w_slot(p, u), (2 * FT + f) * P:(2 * FT + f + 1) * P], start=f == 0, stop=f == FT - 1)
                last.then_inc(eo_mm, 1)

            def put_back(p, b):
                pe.wait_ge(lo_done, number(p) * B + b + 1)
                pe.wait_ge(back_done, number(p) * B + b + 1)
                for k, part in enumerate((eo_hi, eo_lo)):
                    for c in range(GPB):
                        last = pe.matmul(acc[b * GPB + c], part[:, b, :], back[:, b, c * GN:(c + 1) * GN],
                                         start=False, stop=same(p, LAST) and k == 1, skip_group_check=True)
                last.then_inc(back_mm, 1)

            def step(p, u):
                if u + 1 < UNITS:
                    turn(p, u + 1)
                elif not same(p, LAST):
                    turn(after(p), 0)
                gate_up(p, u)
                if u:
                    down(p, u - 1)
                elif not same(p, FIRST):
                    down(before(p), UNITS - 1)
                if u < B and not same(p, FIRST):
                    put_back(before(p), u)

            pe.wait_ge(merge_steps, MERGED)
            turn(FIRST, 0, first=True)
            all_steps(pe, step)
            put_back(LAST, 0)
            down(LAST, UNITS - 1)

            def token_major(g):
                for t in range(GT):
                    last = pe.transpose(room[g][:, t * P:(t + 1) * P], moeT[:, g, t * P:(t + 1) * P], ident)
                last.then_inc(moeT_mm, 1)

            put_back(LAST, 1)
            for g in range(GROUPS - 1):
                pe.wait_ge(moe_act, g + 1)
                token_major(g)
            pe.wait_ge(moe_dve, 1)
            token_major(3)


WARM = 3
LATE_ROUND = 10


def kernel(L0_attn_x, L0_attn_W_q, L0_attn_b_q, L0_attn_W_k, L0_attn_b_k, L0_attn_W_v, L0_attn_b_v, L0_attn_W_o,
           L0_attn_b_o, L0_ffn_gate_w, L0_ffn_Wg, L0_ffn_Wu, L0_ffn_Wd, L0_ffn_Ws_g, L0_ffn_Ws_u, L0_ffn_Ws_d, L0_c,
           L0_wmod):
    import numpy as np
    import concourse.bacc as bacc
    from concourse.bass_utils import run_bass_kernel_spmd

    f32 = np.float32

    def a(v):
        return np.asarray(v)

    def wide(v):
        return np.broadcast_to(a(v)[None, :], (P, D))

    early = np.concatenate([a(L0_c).T, a(L0_attn_b_q)[:, None], np.full((P, 1), LN_EPS, f32), a(L0_wmod)], axis=1)
    attn = np.concatenate([a(L0_attn_W_q).T, a(L0_attn_W_k).T, a(L0_attn_W_v).T, a(L0_attn_W_o).T,
                           wide(L0_attn_b_v), wide(L0_attn_b_o), a(L0_ffn_gate_w).T], axis=1)
    bk_row = np.concatenate([np.tile(a(L0_attn_b_k), (2, 1)), np.array([[1, 0], [-1, 1]], f32)], axis=1)

    eye = np.eye(P, dtype=f32)
    block_of = np.arange(P) // (D // H)
    decay = np.exp(-np.arange(N, dtype=f32) / N).astype(f32)
    const = np.concatenate([
        eye, eye[:, ::-1], (block_of[:, None] == block_of[None, :]).astype(f32),
        (block_of[:, None] == np.arange(H)[None, :]).astype(f32),
        decay.reshape(TPB, P).T, (f32(1e-6) / decay).astype(f32).reshape(TPB, P).T], axis=1)
    iota = np.tile(np.arange(N, dtype=f32), (P, 1))

    def expert_layout(wg, wu, wd):
        n = wg.shape[0]
        gate_up = np.concatenate([wg.transpose(0, 2, 1), wu.transpose(0, 2, 1)], axis=2)
        down = wd.transpose(0, 2, 1).reshape(n, FT, P, D).transpose(0, 2, 1, 3).reshape(n, P, FT * D)
        return np.concatenate([gate_up, down], axis=2)

    wexp = np.concatenate([expert_layout(a(L0_ffn_Wg), a(L0_ffn_Wu), a(L0_ffn_Wd)),
                           expert_layout(a(L0_ffn_Ws_g)[None], a(L0_ffn_Ws_u)[None], a(L0_ffn_Ws_d)[None])], axis=0)

    arrays = {"in_x": a(L0_attn_x), "in_early": early, "in_attn": attn, "in_bk_row": bk_row, "in_const": const,
              "in_iota": iota, "in_wexp": wexp}
    arrays = {k: np.ascontiguousarray(v) for k, v in arrays.items()}

    nc = bacc.Bacc("TRN2", target_bir_lowering=False, num_devices=1)
    args = [nc.dram_tensor(k, v.shape, F32, kind="ExternalInput").ap() for k, v in arrays.items()]
    args.append(nc.dram_tensor("out_y", (B, N, D), F32, kind="ExternalOutput").ap())
    adaln_moe_block(nc, *args)
    r = run_bass_kernel_spmd(nc, [arrays], core_ids=[0])
    return r.results[0]["out_y"]
```

```python
from contextlib import ExitStack

import concourse.bass as bass
from concourse import mybir

P = 128
B, N, D = 2, 1024, 128
H = 16
E, F = 16, 256
CAP = 2 * N // E
FT = F // P
TILES = B * N // P
TPB = N // P
GT = 4
GROUPS = TILES // GT
GPB = GROUPS // B
GN = GT * P
HALF = N // 2
QUARTERS = HALF // P
ROUNDS = CAP // 8
ROWS = 2 * B * E
UNITS = 2 * B
WCOLS = 3 * FT * P
PAIRS = E // 2
PRODUCTS = PAIRS // 2 + 1
WSLOTS = 4
XSLOTS = 2 * UNITS
AHEAD = 6
WARM = 3
FILL = 2
LATE_ROUND = 10
LN_EPS = 1e-5

F32 = mybir.dt.float32
F32R = mybir.dt.float32r
U32 = mybir.dt.uint32
ALU = mybir.AluOpType
ACT = mybir.ActivationFunctionType
AX_X = mybir.AxisListType.X

EARLY = {"c": (0, B), "bq": (B, B + 1), "eps": (B + 1, B + 2), "wmod": (B + 2, B + 2 + 6 * D)}
ATTN = {"wq": (0, 128), "wk": (128, 256), "wv": (256, 384), "wo": (384, 512), "bv": (512, 640),
        "bo": (640, 768), "gate": (768, 784)}
CONST = {"ident": (0, 128), "flip": (128, 256), "blocks": (256, 384), "heads": (384, 400),
         "dec": (400, 408), "epsdec": (408, 416)}
MOD_SA, MOD_CA, MOD_GA, MOD_SB, MOD_CB, MOD_GB = range(6)


def adaln_moe_block(nc, x, early, attn, bk_row, const, iota, wexp, out):
    xhat_rows = [nc.dram_tensor(f"xhat_rows{b}", [N, D], F32, kind="Internal").ap() for b in range(B)]
    base_rows = [nc.dram_tensor(f"base_rows{b}", [N, D], F32, kind="Internal").ap() for b in range(B)]
    x_v = x.rearrange("b (t p) d -> p (b t) d", p=P)
    out_v = out.rearrange("b (t p) d -> p (b t) d", p=P)

    ctx = ExitStack()
    with ctx:
        def sb(name, shape, dt=F32):
            return ctx.enter_context(nc.sbuf_tensor(name, shape, dt))

        def sem(name):
            return ctx.enter_context(nc.semaphore(name))

        x_sb = sb("x_sb", [P, TILES, D])
        xg = sb("xg", [P, TILES, D])
        early_sb = sb("early_sb", [P, EARLY["wmod"][1]])
        attn_sb = sb("attn_sb", [P, ATTN["gate"][1]])
        const_sb = sb("const_sb", [P, CONST["epsdec"][1]])
        bk_sb = sb("bk_sb", [2, D + 2])
        bk_high = sb("bk_high", [2, D], F32R)
        bk_rest = sb("bk_rest", [2, D])
        bk_self = sb("bk_self", [2, D])
        bk_parts = sb("bk_parts", [2, D], F32R)
        ones_two = sb("ones_two", [2, P], F32R)
        ones = sb("ones", [P, GN])
        iota_sb = sb("iota_sb", [P, N])
        wshared = sb("wshared", [P, WCOLS])
        wring = sb("wring", [P, WSLOTS, WCOLS])
        exp_c = sb("exp_c", [P, B])
        exp_c1 = sb("exp_c1", [P, B])
        sig_c = sb("sig_c", [P, B])
        silu_c = sb("silu_c", [P, B])
        mod = sb("mod", [P, 6 * B])
        scale_a = sb("scale_a", [P, B])
        scale_b = sb("scale_b", [P, B])
        gate_turned = sb("gate_turned", [P, 2, B])
        gate_sign = sb("gate_sign", [P, 2, B])
        gate_size = sb("gate_size", [P, 2, B])
        gates = sb("gates", [P, 2, B])
        ga_diag = sb("ga_diag", [P, B, P])
        gb_diag = sb("gb_diag", [P, B, P])
        gb_row = sb("gb_row", [P, B, D])
        wo_gated = sb("wo_gated", [P, B, D])
        bo_gated = sb("bo_gated", [P, B, D])
        stats = sb("stats", [P, 2 * TILES, 6])
        moments = sb("moments", [P, 2 * TILES, 2])
        minus_mean = sb("minus_mean", [P, 2 * TILES])
        std = sb("std", [P, 2 * TILES])
        rstd = sb("rstd", [P, 2 * TILES])
        shift_b = sb("shift_b", [P, TILES])
        xhat = sb("xhat", [P, TILES, D])
        hT = sb("hT", [P, TILES, P])
        qT = sb("qT", [P, TILES, P])
        k_sb = sb("k_sb", [P, 2, GT, D])
        v_sb = sb("v_sb", [P, 2, GT, D + 1])
        ksum = sb("ksum", [P, B])
        kv_full = sb("kv_full", [P, B, D])
        kv_heads = sb("kv_heads", [P, B, D + H])
        den = sb("den", [P, 2, GT, H])
        rden = sb("rden", [P, 2, GT, H])
        att = sb("att", [P, 2, GT, D])
        attT = sb("attT", [P, 2, GT, P])
        top = sb("top", [P, TILES])
        shifted = sb("shifted", [P, TILES, E])
        expd = sb("expd", [P, TILES, E])
        total = sb("total", [P, TILES])
        rtotal = sb("rtotal", [P, TILES])
        scores = sb("scores", [P, QUARTERS, 2, B, E])
        work = sb("work", [ROWS, 2, HALF])
        best = sb("best", [ROWS, CAP])
        where = sb("where", [ROWS, CAP], U32)
        wheref = sb("wheref", [ROWS, CAP])
        lists = sb("lists", [P, 2, 2, B * E])
        first_wins = sb("first_wins", [P, B * E])
        second_place = sb("second_place", [P, B * E])
        place_gap = sb("place_gap", [P, B * E])
        place_add = sb("place_add", [P, B * E])
        chosen_w = sb("chosen_w", [P, E, B])
        chosen_at = sb("chosen_at", [P, E, B])
        chosen_row = sb("chosen_row", [P, E, B], U32)
        gelu_s = sb("gelu_s", [P, 2, FT, GN])
        up_s = sb("up_s", [P, 2, FT, GN])
        hid_s = sb("hid_s", [P, 2, FT, GN])
        xe = sb("xe", [P, XSLOTS, D])
        xeT = sb("xeT", [P, UNITS, P])
        gelu_e = sb("gelu_e", [P, UNITS, FT, P])
        hid_e = sb("hid_e", [P, UNITS, FT, P])
        weighed = sb("weighed", [P, 2, B, D])
        back = sb("back", [P, B, N], F32R)
        eo_full = sb("eo_full", [P, B, D])
        eo_hi = sb("eo_hi", [P, B, D], F32R)
        eo_lo = sb("eo_lo", [P, B, D], F32R)
        base_sb = sb("base_sb", [P, TILES, D])
        moeT = sb("moeT", [P, GROUPS, GN])
        y_sb = sb("y_sb", [P, TILES, D])

        def col(t, table, name):
            a, b = table[name]
            return t[:, a:b]

        def group(t, g):
            return t[:, g * GT:(g + 1) * GT, :]

        def tiled(p, width=P):
            return p.rearrange("p (t q) -> p t q", q=width)

        ident, flip = col(const_sb, CONST, "ident"), col(const_sb, CONST, "flip")
        blocks, heads = col(const_sb, CONST, "blocks"), col(const_sb, CONST, "heads")
        dec, epsdec = col(const_sb, CONST, "dec"), col(const_sb, CONST, "epsdec")
        eps_col = col(early_sb, EARLY, "eps")
        wmod_at = EARLY["wmod"][0]

        def modulation(j, b):
            return mod[:, j * B + b:j * B + b + 1]

        def gate_col(which, b):
            return gates[:, which, b:b + 1]

        psum = ctx.enter_context(nc.psum_tensor("psum", [P, 8 * GN], F32))

        def banks(i, n=1):
            return psum[:, i * GN:(i + n) * GN]

        q_ps, k_ps, v_ps = banks(0), banks(1), banks(2)
        kv_ps = (banks(3), banks(0))
        t_ps = (banks(4), banks(5))
        attT_ps = banks(5)
        route_ps = (banks(4), banks(6), banks(7), banks(4))
        o_ps = (banks(6, 2), banks(6, 2), banks(1, 2), banks(6, 2))
        y_ps = (banks(3), banks(3), banks(0), banks(3))
        mod_ps, ga_ps, warm_ps = banks(6), banks(7), banks(3)
        gb_ps, scoresT_ps = banks(5), banks(4)

        def norm_ps(n):
            return t_ps[n % 2] if n < GROUPS else route_ps[n - GROUPS]

        acc = (banks(0), banks(3), banks(5), banks(4))
        room = (banks(1), banks(2), banks(6), banks(7))
        hid_ps = room
        merge_ps = room[3]
        gu_ps, xeT_ps, eo_ps = room[0:2], room[2], room[3]

        x_in = [sem(f"x_in{g}") for g in range(GROUPS)]
        early_in, attn_in, const_in, bk_in = sem("early_in"), sem("attn_in"), sem("const_in"), sem("bk_in")
        bk_steps = sem("bk_steps")
        iota_in, shared_in = sem("iota_in"), sem("shared_in")
        w_in = [sem(f"w_in{n}") for n in range(WSLOTS)]
        rows_out, base_out = sem("rows_out"), sem("base_out")
        rows_in = [sem(f"rows_in{n}") for n in range(XSLOTS)]
        scattered = [sem(f"scattered{b}") for b in range(B)]
        base_in = [sem(f"base_in{g}") for g in range(GROUPS)]
        y_out = sem("y_out")

        ones_set = sem("ones_set")
        exp_c_done, silu_steps = sem("exp_c_done"), sem("silu_steps")
        mod_mm, ga_mm, mod_steps, gate_steps = sem("mod_mm"), sem("ga_mm"), sem("mod_steps"), sem("gate_steps")
        gadiag_done, gated_done = sem("gadiag_done"), sem("gated_done")
        gbdiag_done, gb_mm, gbrow_done = sem("gbdiag_done"), sem("gb_mm"), sem("gbrow_done")
        xg_done = sem("xg_done")
        stats_done, moments_done = sem("stats_done"), sem("moments_done")
        std_done, rstd_done = sem("std_done"), sem("rstd_done")
        minus_mean_done, shift_b_done, xhat_act = sem("minus_mean_done"), sem("shift_b_done"), sem("xhat_act")
        xhat_dve, xhat_pool = sem("xhat_dve"), sem("xhat_pool")
        xT_mm, hT_done = sem("xT_mm"), sem("hT_done")
        q_mm, k_mm, v_mm, kv_mm = sem("q_mm"), sem("k_mm"), sem("v_mm"), sem("kv_mm")
        q_done, k_done, v_done = sem("q_done"), sem("k_done"), sem("v_done")
        ksum_done, kvfull_done, kv_done = sem("ksum_done"), sem("kvfull_done"), sem("kv_done")
        o_mm, den_done, rden_done, att_done = sem("o_mm"), sem("den_done"), sem("rden_done"), sem("att_done")
        attT_mm, attT_done = sem("attT_mm"), sem("attT_done")
        y_mm, x1_done = sem("y_mm"), sem("x1_done")
        logit_mm = sem("logit_mm")
        top_done, shift_done, expd_done = sem("top_done"), sem("shift_done"), sem("expd_done")
        total_done, rtotal_done, score_done = sem("total_done"), sem("rtotal_done"), sem("score_done")
        scoresT_mm = sem("scoresT_mm")
        max_done, place_done, strike_done, wheref_done = (sem("max_done"), sem("place_done"), sem("strike_done"),
                                                          sem("wheref_done"))
        lists_mm, merge_steps, flip_mm = sem("lists_mm"), sem("merge_steps"), sem("flip_mm")
        sg_mm, su_mm = sem("sg_mm"), sem("su_mm")
        sgelu_done, sup_done, shid_done, sdown_mm = sem("sgelu_done"), sem("sup_done"), sem("shid_done"), sem("sdown_mm")
        xeT_mm, xeT_done, gu_mm = sem("xeT_mm"), sem("xeT_done"), sem("gu_mm")
        gelu_done, hid_done, eo_mm = sem("gelu_done"), sem("hid_done"), sem("eo_mm")
        weighed_done, lo_done = sem("weighed_done"), sem("lo_done")
        hi_done, back_done, back_mm = sem("hi_done"), sem("back_done"), sem("back_mm")
        moe_act, moe_dve, moeT_mm, y_done = sem("moe_act"), sem("moe_dve"), sem("moeT_mm"), sem("y_done")

        MOD_COPIED, MOD_SCALES = 1, 3
        LISTED, PLACES_CHOSEN, MERGED = 1, 7, 8
        BE = B * E


        def halves_b(g):
            return (xhat_act, (g + 1) * GT // 2) if g < GROUPS - 1 else (xhat_dve, (GROUPS + 1) * GT // 2)

        def number(p):
            k, odd = p
            return k * 2 + odd

        def before(p):
            k, odd = p
            return (k, 0) if odd else (k - 1, 1)

        def after(p):
            k, odd = p
            return (k + 1, 0) if odd else (k, 1)

        def x_slot(p, u):
            return p[1] * UNITS + u

        def w_slot(p, u):
            return p[1] * 2 + u // B

        FIRST, LAST = (0, 0), (PAIRS // 2 - 1, 1)

        def same(p, q):
            return isinstance(p[0], int) and p == q

        def by_product(p, u):
            return u >= B and (p[1] == 1 or same(p, FIRST))

        def products_before(p):
            return 0 if same(p, FIRST) else p[0] + 1

        def scatters_before(p, u):
            k, odd = p
            return u // B if same(p, FIRST) else k * 3 + odd * 2 + u // B - 1

        def all_steps(engine, step):
            for u in range(UNITS):
                step(FIRST, u)
            for u in range(UNITS - 1):
                step(after(FIRST), u)
            with engine.Fori(0, PAIRS // 2 - 1) as k:
                step((k, 1), UNITS - 1)
                for u in range(UNITS):
                    step((k + 1, 0), u)
                for u in range(UNITS - 1):
                    step((k + 1, 1), u)
            step(LAST, UNITS - 1)

        block = ctx.enter_context(nc.Block())

        @block.sync
        def _(sp):
            sp.dma_start(group(x_sb, 0), group(x_v, 0)).then_inc(x_in[0], 16)
            sp.dma_start(early_sb[:, :], early).then_inc(early_in, 16)
            sp.dma_start(bk_sb[:, :], bk_row).then_inc(bk_in, 16)
            sp.dma_start(group(x_sb, 1), group(x_v, 1)).then_inc(x_in[1], 16)
            sp.dma_start(const_sb[:, :], const).then_inc(const_in, 16)
            sp.dma_start(attn_sb[:, :], attn).then_inc(attn_in, 16)
            for g in range(2, GROUPS):
                sp.dma_start(group(x_sb, g), group(x_v, g)).then_inc(x_in[g], 16)
            sp.dma_start(wshared[:, :], wexp[E, :, :]).then_inc(shared_in, 16)
            sp.dma_start(iota_sb[:, :], iota).then_inc(iota_in, 16)
            for n in range(WSLOTS):
                sp.dma_start(wring[:, n, :], wexp[n, :, :]).then_inc(w_in[n], 16)
            for g in range(GROUPS):
                rows = slice((g % GPB) * GN, (g % GPB + 1) * GN)
                sp.wait_ge(x1_done, g + 1)
                sp.dma_start(base_rows[g // GPB][rows, :].rearrange("(t p) d -> p t d", p=P), group(xg, g)).then_inc(base_out, 16)
                sp.wait_ge(*halves_b(g))
                sp.wait_ge(xhat_pool, (GROUPS + g + 1) * GT // 2)
                sp.dma_start(xhat_rows[g // GPB][rows, :].rearrange("(t p) d -> p t d", p=P), group(xhat, g)).then_inc(rows_out, 16)
            with sp.Fori(1, PAIRS // 2) as k:
                for n in range(WSLOTS):
                    sp.wait_ge(eo_mm, (k - 1) * 2 * UNITS + B * (n + 1))
                    sp.dma_start(wring[:, n, :], wexp[bass.ds(k * WSLOTS + n, 1), :, :].rearrange("a p n -> p (a n)")).then_inc(w_in[n], 16)
            for g in range(GROUPS):
                if g % GPB == 0:
                    sp.wait_ge(scattered[g // GPB], 16 * (E - PRODUCTS))
                rows = slice((g % GPB) * GN, (g % GPB + 1) * GN)
                sp.dma_start(group(base_sb, g), base_rows[g // GPB][rows, :].rearrange("(t p) d -> p t d", p=P)).then_inc(base_in[g], 16)
            for g in range(GROUPS):
                sp.wait_ge(y_done, g + 1)
                sp.dma_start(group(out_v, g), group(y_sb, g)).then_inc(y_out, 16)
            sp.wait_ge(y_out, 16 * GROUPS)

        @block.gpsimd
        def _(pool):
            def normalise(n, src):
                g = n % GROUPS
                pool.wait_ge(minus_mean_done, n + 1)
                pool.wait_ge(rstd_done, n + 1)
                if n >= GROUPS:
                    pool.wait_ge(xT_mm, g + 1)
                for t in range(GT // 2):
                    m = n * GT + t
                    pool.tensor_scalar(xhat[:, g * GT + t, :], src[:, g * GT + t, :], minus_mean[:, m:m + 1], rstd[:, m:m + 1],
                                       op0=ALU.add, op1=ALU.mult).then_inc(xhat_pool, 1)

            normalise(0, x_sb)
            pool.wait_ge(bk_in, 16)
            pool.tensor_scalar(bk_high[:, :], bk_sb[:, 0:D], 1.0, 0.0, op0=ALU.mult, op1=ALU.add).then_inc(bk_steps, 1)
            pool.tensor_scalar(bk_self[:, :], bk_sb[:, 0:D], bk_sb[:, D + 1:D + 2], 0.0, op0=ALU.mult, op1=ALU.add).then_inc(bk_steps, 1)
            pool.wait_ge(bk_steps, 1)
            pool.tensor_scalar(bk_rest[:, :], bk_high[:, :].bitcast(F32), bk_sb[:, D:D + 1], 0.0, op0=ALU.mult, op1=ALU.add)\
                .then_inc(bk_steps, 1)
            pool.wait_ge(bk_steps, 3)
            pool.tensor_tensor(bk_parts[:, :], bk_self[:, :], bk_rest[:, :], op=ALU.add).then_inc(bk_steps, 1)
            for n in range(1, GROUPS):
                normalise(n, x_sb)
            pool.wait_ge(gated_done, 2)
            for g in range(GROUPS):
                pool.tensor_tensor(group(xg, g), group(x_sb, g),
                                   bo_gated[:, g // GPB:g // GPB + 1, :].to_broadcast([P, GT, D]),
                                   op=ALU.add).then_inc(xg_done, 1)
            pool.wait_ge(gate_steps, 4)
            for b in range(B):
                pool.tensor_scalar(gb_diag[:, b, :], ident, gate_col(1, b), 0.0, op0=ALU.mult, op1=ALU.add).then_inc(gbdiag_done, 1)
            for n in range(GROUPS, 2 * GROUPS):
                normalise(n, xg)
            for c in range(GROUPS):
                for f in range(FT):
                    n = c * FT + f + 1
                    pool.wait_ge(sgelu_done, n)
                    pool.wait_ge(sup_done, n)
                    if c >= 2:
                        pool.wait_ge(sdown_mm, c - 1)
                    pool.tensor_tensor(hid_s[:, c % 2, f, :], gelu_s[:, c % 2, f, :], up_s[:, c % 2, f, :],
                                       op=ALU.mult).then_inc(shid_done, 1)

            def expert_batch(n):
                return n // B, n % B

            def gather(n):
                e, b = expert_batch(n)
                if n >= XSLOTS:
                    pool.wait_ge(xeT_mm, n - XSLOTS + 1)
                pool.indirect_dma_start(
                    out=xe[:, n % XSLOTS, :], out_offset=None, in_=xhat_rows[b],
                    in_offset=bass.IndirectOffsetOnAxis(ap=chosen_row[:, e, b:b + 1], axis=0)).then_inc(rows_in[n % XSLOTS], 16)

            def scatter(p, u):
                e, b = number(p) * 2 + u // B, u % B
                if scatters_before(p, u):
                    pool.wait_ge(scattered[b], 16 * scatters_before(p, u))
                pool.wait_ge(weighed_done, scatters_before(p, u) * B + b + 1)
                pool.indirect_dma_start(
                    out=base_rows[b], out_offset=bass.IndirectOffsetOnAxis(ap=chosen_row[:, e, b:b + 1], axis=0),
                    in_=weighed[:, u // B, b, :], in_offset=None, compute_op=ALU.add).then_inc(scattered[b], 16)

            pool.wait_ge(rows_out, 16 * GROUPS)
            pool.wait_ge(base_out, 16 * GROUPS)
            pool.wait_ge(merge_steps, PLACES_CHOSEN)
            for n in range(-AHEAD, B * E):
                if n + AHEAD < B * E:
                    gather(n + AHEAD)
                if n >= 1:
                    i, u = (n - 1) // UNITS, (n - 1) % UNITS
                    if not by_product((i // 2, i % 2), u):
                        scatter((i // 2, i % 2), u)

        @block.scalar
        def _(act):
            act.wait_ge(early_in, 16)
            act.activation(exp_c[:, :], col(early_sb, EARLY, "c"), ACT.Exp, scale=-1.0).then_inc(exp_c_done, 1)

            def norm_std(n):
                act.wait_ge(moments_done, (n + 1) * GT)
                act.activation(std[:, n * GT:(n + 1) * GT], moments[:, n * GT:(n + 1) * GT, 1], ACT.Sqrt,
                               bias=eps_col).then_inc(std_done, 1)

            def normalise_b(g):
                n = GROUPS + g
                act.wait_ge(shift_b_done, g + 1)
                act.wait_ge(xT_mm, g + 1)
                for t in range(GT // 2, GT):
                    m = n * GT + t
                    act.activation(xhat[:, g * GT + t, :], xg[:, g * GT + t, :], ACT.Identity, scale=rstd[:, m:m + 1],
                                   bias=shift_b[:, g * GT + t:g * GT + t + 1]).then_inc(xhat_act, 1)

            def modulated(n, scale, shift):
                g = n % GROUPS
                act.wait_ge(xT_mm, n + 1)
                act.activation(group(hT, g), tiled(norm_ps(n)), ACT.Identity, scale=scale[:, g // GPB:g // GPB + 1],
                               bias=modulation(shift, g // GPB)).then_inc(hT_done, 1)

            def modulated_a(g):
                if g == 0:
                    act.wait_ge(mod_steps, MOD_SCALES)
                modulated(g, scale_a, MOD_SA)

            def query(g):
                act.wait_ge(q_mm, g + 1)
                act.activation(group(qT, g), tiled(q_ps), ACT.Relu, bias=col(early_sb, EARLY, "bq")).then_inc(q_done, 1)

            def key(g):
                act.wait_ge(k_mm, g + 1)
                if g >= 2:
                    act.wait_ge(kv_mm, g - 1)
                act.activation(k_sb[:, g % 2, :, :], tiled(k_ps), ACT.Relu).then_inc(k_done, 1)

            norm_std(0)
            norm_std(1)
            modulated_a(0)
            norm_std(2)
            modulated_a(1)
            norm_std(3)
            for g in range(GROUPS):
                query(g)
                key(g)
                if g + 2 < GROUPS:
                    modulated_a(g + 2)

            def attention_out(g):
                act.wait_ge(attT_mm, g + 1)
                if g >= 2:
                    act.wait_ge(y_mm, g - 1)
                act.activation(attT[:, g % 2, :, :], tiled(attT_ps), ACT.Copy).then_inc(attT_done, 1)

            def modulated_b(g):
                modulated(GROUPS + g, scale_b, MOD_SB)

            attention_out(0)
            attention_out(1)
            norm_std(GROUPS)
            normalise_b(0)
            modulated_b(0)
            attention_out(2)
            attention_out(3)
            norm_std(GROUPS + 1)
            normalise_b(1)
            norm_std(GROUPS + 2)
            modulated_b(1)
            normalise_b(2)
            norm_std(GROUPS + 3)
            modulated_b(2)
            modulated_b(GROUPS - 1)
            for b in range(B):
                act.wait_ge(shift_done, (b + 1) * GPB)
                at = slice(b * TPB, (b + 1) * TPB)
                act.activation(expd[:, at, :], shifted[:, at, :], ACT.Exp).then_inc(expd_done, 1)
            act.wait_ge(gb_mm, 1)
            act.activation(gb_row[:, :, :], tiled(gb_ps[:, 0:B * D]), ACT.Copy).then_inc(gbrow_done, 1)
            for c in range(GROUPS):
                for f in range(FT):
                    n = c * FT + f + 1
                    act.wait_ge(sg_mm, n)
                    if c >= 2:
                        act.wait_ge(shid_done, n - 2 * FT)
                    act.activation(gelu_s[:, c % 2, f, :], hid_ps[f], ACT.Gelu).then_inc(sgelu_done, 1)
                    act.wait_ge(su_mm, n)
                    act.activation(up_s[:, c % 2, f, :], hid_ps[FT + f], ACT.Copy).then_inc(sup_done, 1)

            def evacuate_x(p, u):
                b = u % B
                act.wait_ge(xeT_mm, number(p) * UNITS + u + 1)
                act.activation(xeT[:, u, :], xeT_ps[:, u * P:(u + 1) * P], ACT.Identity,
                               scale=scale_b[:, b:b + 1], bias=modulation(MOD_SB, b)).then_inc(xeT_done, 1)

            def gelu(p, u):
                act.wait_ge(gu_mm, number(p) * UNITS + u + 1)
                act.activation(gelu_e[:, u, :, :], tiled(gu_ps[u % 2][:, 0:F]), ACT.Gelu).then_inc(gelu_done, 1)

            def high_part(p, u):
                b = u % B
                act.wait_ge(eo_mm, number(p) * UNITS + u + 1)
                if not same(p, FIRST):
                    act.wait_ge(back_mm, (products_before(p) - 1) * B + b + 1)
                act.activation(eo_hi[:, b, :], eo_ps[:, 0:D], ACT.Copy,
                               scale=chosen_w[:, bass.ds(number(p) * 2 + 1, 1), b]).then_inc(hi_done, 1)
                act.activation(eo_full[:, b, :], eo_ps[:, 0:D], ACT.Copy,
                               scale=chosen_w[:, bass.ds(number(p) * 2 + 1, 1), b]).then_inc(hi_done, 1)

            def step(p, u):
                if u + 1 < UNITS:
                    evacuate_x(p, u + 1)
                elif not same(p, LAST):
                    evacuate_x(after(p), 0)
                gelu(p, u)
                if u == UNITS - 1:
                    if by_product(p, u - 1):
                        high_part(p, u - 1)
                elif u == 0 and not same(p, FIRST) and by_product(before(p), UNITS - 1):
                    high_part(before(p), UNITS - 1)

            def gate_moe(g):
                act.wait_ge(back_mm, B * (PRODUCTS - 1) + g // GPB + 1)
                act.activation(moeT[:, g, :], acc[g], ACT.Copy, scale=gate_col(1, g // GPB)).then_inc(moe_act, 1)

            act.wait_ge(merge_steps, MERGED)
            evacuate_x(FIRST, 0)
            all_steps(act, step)
            high_part(LAST, UNITS - 1)
            for g in range(1, GROUPS):
                gate_moe(g)

        @block.vector
        def _(dve):
            dve.memset(ones[:, :], 1.0).then_inc(ones_set, 1)
            dve.wait_ge(ones_set, 1)
            dve.tensor_copy(ones_two[:, :], ones[0:2, 0:P]).then_inc(ones_set, 1)

            def norm_stats(n, src):
                g = n % GROUPS
                for t in range(GT):
                    dve.bn_stats(stats[:, n * GT + t, :], src[:, g * GT + t, :]).then_inc(stats_done, 1)
                for t in range(GT):
                    dve.wait_ge(stats_done, n * GT + t + 1)
                    dve.bn_aggr(moments[:, n * GT + t, :], stats[:, n * GT + t, :]).then_inc(moments_done, 1)

            def norm_factors(n):
                at = slice(n * GT, (n + 1) * GT)
                dve.wait_ge(moments_done, (n + 1) * GT)
                dve.tensor_scalar_mul(minus_mean[:, at], moments[:, at, 0], -1.0).then_inc(minus_mean_done, 1)
                dve.wait_ge(std_done, n + 1)
                dve.reciprocal(rstd[:, at], std[:, at]).then_inc(rstd_done, 1)
                dve.wait_ge(rstd_done, n + 1)

            def normalise(n, src):
                g = n % GROUPS
                norm_factors(n)
                if n >= GROUPS:
                    dve.wait_ge(xT_mm, g + 1)
                for t in range(GT // 2, GT):
                    m = n * GT + t
                    dve.tensor_scalar(xhat[:, g * GT + t, :], src[:, g * GT + t, :], minus_mean[:, m:m + 1], rstd[:, m:m + 1],
                                      op0=ALU.add, op1=ALU.mult).then_inc(xhat_dve, 1)

            def norm_factors_b(g):
                at = slice((GROUPS + g) * GT, (GROUPS + g + 1) * GT)
                norm_factors(GROUPS + g)
                dve.tensor_tensor(shift_b[:, g * GT:(g + 1) * GT], minus_mean[:, at], rstd[:, at], op=ALU.mult)\
                    .then_inc(shift_b_done, 1)

            dve.wait_ge(x_in[0], 16)
            norm_stats(0, x_sb)
            dve.wait_ge(exp_c_done, 1)
            dve.tensor_scalar_add(exp_c1[:, :], exp_c[:, :], 1.0).then_inc(silu_steps, 1)
            dve.wait_ge(silu_steps, 1)
            dve.reciprocal(sig_c[:, :], exp_c1[:, :]).then_inc(silu_steps, 1)
            dve.wait_ge(silu_steps, 2)
            dve.tensor_tensor(silu_c[:, :], col(early_sb, EARLY, "c"), sig_c[:, :], op=ALU.mult).then_inc(silu_steps, 1)
            normalise(0, x_sb)
            dve.wait_ge(x_in[1], 16)
            norm_stats(1, x_sb)
            dve.wait_ge(mod_mm, 1)
            dve.tensor_copy(mod[:, :], mod_ps[:, 0:6 * B]).then_inc(mod_steps, 1)
            dve.wait_ge(mod_steps, MOD_COPIED)
            dve.tensor_scalar_add(scale_a[:, :], mod[:, MOD_CA * B:(MOD_CA + 1) * B], 1.0).then_inc(mod_steps, 1)
            dve.tensor_scalar_add(scale_b[:, :], mod[:, MOD_CB * B:(MOD_CB + 1) * B], 1.0).then_inc(mod_steps, 1)
            normalise(1, x_sb)
            dve.wait_ge(x_in[2], 16)
            norm_stats(2, x_sb)
            normalise(2, x_sb)
            dve.wait_ge(x_in[3], 16)
            norm_stats(3, x_sb)
            normalise(3, x_sb)
            raw = mod[:, :].rearrange("p (j b) -> p j b", b=B)[:, MOD_GA:MOD_GB + 1:MOD_GB - MOD_GA, :]
            dve.tensor_scalar(gate_sign[:, :, :], raw, 0.0, 2.0, op0=ALU.is_ge, op1=ALU.mult).then_inc(gate_steps, 1)
            dve.tensor_scalar(gate_turned[:, :, :], raw, -1.0, 0.25, op0=ALU.mult, op1=ALU.max).then_inc(gate_steps, 1)
            dve.wait_ge(gate_steps, 2)
            dve.scalar_tensor_tensor(gate_size[:, :, :], raw, 0.25, gate_turned[:, :, :], op0=ALU.max, op1=ALU.max)\
                .then_inc(gate_steps, 1)
            dve.wait_ge(gate_steps, 3)
            dve.scalar_tensor_tensor(gates[:, :, :], gate_sign[:, :, :], -1.0, gate_size[:, :, :], op0=ALU.add, op1=ALU.mult)\
                .then_inc(gate_steps, 1)
            dve.wait_ge(gate_steps, 4)
            dve.wait_ge(const_in, 16)
            for b in range(B):
                dve.tensor_scalar_mul(ga_diag[:, b, :], ident, gate_col(0, b)).then_inc(gadiag_done, 1)
            def heads_of(b):
                dve.wait_ge(kv_mm, (b + 1) * GPB)
                dve.tensor_copy(ksum[:, b:b + 1], kv_ps[b][:, D:D + 1]).then_inc(ksum_done, 1)
                dve.wait_ge(ksum_done, b + 1)
                dve.scalar_tensor_tensor(kv_full[:, b, :], col(attn_sb, ATTN, "bv"), ksum[:, b:b + 1],
                                         kv_ps[b][:, 0:D], op0=ALU.mult, op1=ALU.add).then_inc(kvfull_done, 1)
                dve.tensor_scalar_mul(kv_heads[:, b, D:D + H], heads, ksum[:, b:b + 1]).then_inc(kv_done, 1)
                dve.wait_ge(kvfull_done, b + 1)
                dve.tensor_tensor(kv_heads[:, b, 0:D], kv_full[:, b, :], blocks, op=ALU.mult).then_inc(kv_done, 1)

            def value(g):
                if g >= 2:
                    dve.wait_ge(kv_mm, g - 1)
                dec_g = dec[:, (g % GPB) * GT:(g % GPB + 1) * GT].unsqueeze(2)
                dve.tensor_copy(v_sb[:, g % 2, :, D:D + 1], dec_g).then_inc(v_done, 1)
                dve.wait_ge(v_mm, g + 1)
                dve.tensor_tensor(v_sb[:, g % 2, :, 0:D], tiled(v_ps), dec_g.to_broadcast([P, GT, D]),
                                  op=ALU.mult).then_inc(v_done, 1)

            def divide(g):
                s = g % 2
                dve.wait_ge(o_mm, g + 1)
                if g >= 2:
                    dve.wait_ge(attT_mm, g - 1)
                eps_g = epsdec[:, (g % GPB) * GT:(g % GPB + 1) * GT]
                o = tiled(o_ps[g], 256)
                dve.tensor_tensor(den[:, s, :, :], o[:, :, D:D + H], eps_g.unsqueeze(2).to_broadcast([P, GT, H]),
                                  op=ALU.add).then_inc(den_done, 1)
                dve.wait_ge(den_done, g + 1)
                dve.reciprocal(rden[:, s, :, :], den[:, s, :, :]).then_inc(rden_done, 1)
                dve.wait_ge(rden_done, g + 1)
                dve.tensor_tensor(att[:, s, :, :].rearrange("p t (h k) -> p t h k", h=H),
                                  o[:, :, 0:D].rearrange("p t (h k) -> p t h k", h=H),
                                  rden[:, s, :, :].unsqueeze(3).to_broadcast([P, GT, H, D // H]),
                                  op=ALU.mult).then_inc(att_done, 1)

            def residual(g):
                dve.wait_ge(y_mm, g + 1)
                dve.wait_ge(xg_done, g + 1)
                dve.tensor_tensor(group(xg, g), group(xg, g), tiled(y_ps[g]), op=ALU.add).then_inc(x1_done, 1)
                dve.wait_ge(x1_done, g + 1)

            def soften_in(g):
                at = slice(g * GT, (g + 1) * GT)
                logits = tiled(route_ps[g][:, 0:GT * E], E)
                dve.wait_ge(logit_mm, g + 1)
                dve.tensor_reduce(top[:, at], logits, axis=AX_X, op=ALU.max).then_inc(top_done, 1)
                dve.wait_ge(top_done, g + 1)
                dve.tensor_tensor(shifted[:, at, :], logits, top[:, at].unsqueeze(2).to_broadcast([P, GT, E]),
                                  op=ALU.subtract).then_inc(shift_done, 1)

            def soften_out():
                for b in range(B):
                    at = slice(b * TPB, (b + 1) * TPB)
                    dve.wait_ge(expd_done, b + 1)
                    dve.tensor_reduce(total[:, at], expd[:, at, :], axis=AX_X, op=ALU.add).then_inc(total_done, 1)
                dve.wait_ge(total_done, B)
                dve.reciprocal(rtotal[:, :], total[:, :]).then_inc(rtotal_done, 1)
                dve.wait_ge(rtotal_done, 1)
                for b in range(B):
                    at = slice(b * TPB, (b + 1) * TPB)
                    dve.tensor_tensor(scores[:, :, :, b, :], expd[:, at, :].rearrange("p (h q) e -> p q h e", h=2),
                                      rtotal[:, at].rearrange("p (h q) -> p q h", h=2).unsqueeze(3).to_broadcast([P, QUARTERS, 2, E]),
                                      op=ALU.mult).then_inc(score_done, 1)

            value(0)
            value(1)
            dve.wait_ge(ga_mm, 1)
            dve.wait_ge(attn_in, 16)
            for name, gated in (("wo", wo_gated), ("bo", bo_gated)):
                dve.tensor_tensor(gated[:, :, :], tiled(ga_ps[:, 0:B * D]),
                                  col(attn_sb, ATTN, name).unsqueeze(1).to_broadcast([P, B, D]),
                                  op=ALU.mult).then_inc(gated_done, 1)
            heads_of(0)
            value(2)
            divide(0)
            divide(1)
            value(3)
            residual(0)
            norm_stats(GROUPS, xg)
            heads_of(1)
            norm_factors_b(0)
            residual(1)
            divide(2)
            divide(3)
            norm_stats(GROUPS + 1, xg)
            residual(2)
            norm_factors_b(1)
            norm_stats(GROUPS + 2, xg)
            residual(3)
            norm_factors_b(2)
            norm_stats(GROUPS + 3, xg)
            soften_in(0)
            normalise(GROUPS + 3, xg)
            soften_in(1)
            soften_in(2)
            soften_in(3)
            soften_out()

            dve.wait_ge(scoresT_mm, 1)
            for r in range(ROUNDS):
                at = slice(8 * r, 8 * r + 8)
                now, then = work[:, r % 2, :] if r else scoresT_ps[0:ROWS, :], work[:, (r + 1) % 2, :]
                if r:
                    dve.wait_ge(strike_done, r)
                dve.max(best[:, at], now).then_inc(max_done, 1)
                dve.wait_ge(max_done, r + 1)
                if r < ROUNDS - 1:
                    if r:
                        dve.wait_ge(place_done, r)
                    dve.match_replace(then, best[:, at], now, -1.0).then_inc(strike_done, 1)
                dve.max_index(where[:, at], best[:, at], now).then_inc(place_done, 1)
            dve.wait_ge(place_done, ROUNDS)
            dve.tensor_copy(wheref[:, :], where[:, :]).then_inc(wheref_done, 1)
            dve.wait_ge(lists_mm, 1)
            dve.tensor_copy(lists[:, :, :, :], merge_ps[:, 0:4 * BE].rearrange("p (k h r) -> p k h r", k=2, h=2))\
                .then_inc(merge_steps, 1)
            dve.wait_ge(flip_mm, 1)
            flipped = merge_ps[:, 4 * BE:6 * BE].rearrange("p (k r) -> p k r", k=2)

            def by_batch(a):
                return a.rearrange("p (b e) -> p b e", b=B)

            dve.tensor_scalar_add(second_place[:, :], flipped[:, 1, :], float(HALF)).then_inc(merge_steps, 1)
            dve.tensor_tensor(first_wins[:, :], lists[:, 0, 0, :], flipped[:, 0, :], op=ALU.is_ge).then_inc(merge_steps, 1)
            dve.wait_ge(merge_steps, LISTED + 1)
            dve.tensor_tensor(place_gap[:, :], lists[:, 1, 0, :], second_place[:, :], op=ALU.subtract).then_inc(merge_steps, 1)
            dve.tensor_tensor(chosen_w[:, :, :].rearrange("p e b -> p b e"), by_batch(lists[:, 0, 0, :]),
                              by_batch(flipped[:, 0, :]), op=ALU.max).then_inc(merge_steps, 1)
            dve.wait_ge(merge_steps, LISTED + 3)
            dve.tensor_tensor(place_add[:, :], place_gap[:, :], first_wins[:, :], op=ALU.mult).then_inc(merge_steps, 1)
            dve.wait_ge(merge_steps, LISTED + 5)
            for chosen in (chosen_row, chosen_at):
                dve.tensor_tensor(chosen[:, :, :].rearrange("p e b -> p b e"), by_batch(second_place[:, :]),
                                  by_batch(place_add[:, :]), op=ALU.add).then_inc(merge_steps, 1)

            def way_back(p, b):
                if not same(p, FIRST):
                    dve.wait_ge(back_mm, (products_before(p) - 1) * B + b + 1)
                dve.tensor_scalar(back[:, b, :], iota_sb[:, :], chosen_at[:, bass.ds(number(p) * 2 + 1, 1), b], None,
                                  op0=ALU.is_equal).then_inc(back_done, 1)

            def hidden(p, u):
                dve.wait_ge(gelu_done, number(p) * UNITS + u + 1)
                dve.tensor_tensor(hid_e[:, u, :, :], gelu_e[:, u, :, :], tiled(gu_ps[u % 2][:, F:2 * F]),
                                  op=ALU.mult).then_inc(hid_done, 1)

            def take_out(p, u):
                b = u % B
                w = chosen_w[:, bass.ds(number(p) * 2 + u // B, 1), b]
                if by_product(p, u):
                    dve.wait_ge(hi_done, (products_before(p) * B + b + 1) * 2)
                    dve.tensor_tensor(eo_lo[:, b, :], eo_full[:, b, :], eo_hi[:, b, :].bitcast(F32),
                                      op=ALU.subtract).then_inc(lo_done, 1)
                else:
                    if not same(p, FIRST):
                        other_slot = u >= B or (p[1] == 1 and not same(p, after(FIRST)))
                        dve.wait_ge(scattered[b], (scatters_before(p, u) - other_slot) * 16)
                    dve.wait_ge(eo_mm, number(p) * UNITS + u + 1)
                    dve.scalar_tensor_tensor(weighed[:, u // B, b, :], eo_ps[:, 0:D], w, gb_row[:, b, :],
                                             op0=ALU.mult, op1=ALU.mult).then_inc(weighed_done, 1)

            def step(p, u):
                hidden(p, u)
                if u:
                    take_out(p, u - 1)
                elif not same(p, FIRST):
                    take_out(before(p), UNITS - 1)
                if by_product(p, u):
                    way_back(p, u % B)

            dve.wait_ge(iota_in, 16)
            dve.wait_ge(gbrow_done, 1)
            dve.wait_ge(merge_steps, MERGED)
            all_steps(dve, step)
            dve.wait_ge(back_mm, B * (PRODUCTS - 1) + 1)
            dve.tensor_scalar_mul(moeT[:, 0, :], acc[0], gate_col(1, 0)).then_inc(moe_dve, 1)
            take_out(LAST, UNITS - 1)

            def finish(g):
                dve.wait_ge(base_in[g], 16)
                dve.wait_ge(moeT_mm, g + 1)
                dve.tensor_tensor(group(y_sb, g), group(base_sb, g), tiled(room[g]), op=ALU.add).then_inc(y_done, 1)

            for g in range(GROUPS):
                finish(g)

        @block.tensor
        def _(pe):
            pe.wait_ge(ones_set, 1)
            for _ in range(WARM):
                pe.matmul(warm_ps, ones[:, 0:P], ones[:, :], start=True, stop=True)
            pe.wait_ge(silu_steps, 3)
            pe.wait_ge(early_in, 16)
            for j in range(6):
                last = pe.matmul(mod_ps[:, j * B:(j + 1) * B], early_sb[:, wmod_at + j * D:wmod_at + (j + 1) * D],
                                 silu_c[:, :], start=True, stop=True)
            last.then_inc(mod_mm, 1)

            def transposes(n):
                g = n % GROUPS
                pe.wait_ge(xhat_pool, (n + 1) * GT // 2)
                for t in range(GT):
                    if t == GT // 2:
                        if n < GROUPS:
                            pe.wait_ge(xhat_dve, (n + 1) * GT // 2)
                        else:
                            pe.wait_ge(*halves_b(g))
                    last = pe.transpose(norm_ps(n)[:, t * P:(t + 1) * P], xhat[:, g * GT + t, :], ident)
                last.then_inc(xT_mm, 1)

            def query(g):
                pe.wait_ge(hT_done, g + 1)
                if g:
                    pe.wait_ge(q_done, g)
                pe.matmul(tiled(q_ps), col(attn_sb, ATTN, "wq"), group(hT, g), start=True, stop=True).then_inc(q_mm, 1)

            def key(g):
                if g:
                    pe.wait_ge(k_done, g)
                pe.matmul(tiled(k_ps), ones_two[:, :], bk_parts[:, :].unsqueeze(1).to_broadcast([2, GT, D]), start=True, stop=False)
                for t in range(GT):
                    last = pe.matmul(k_ps[:, t * D:(t + 1) * D], hT[:, g * GT + t, :], col(attn_sb, ATTN, "wk"),
                                     start=False, stop=t == GT - 1)
                last.then_inc(k_mm, 1)

            def value(g):
                if g:
                    pe.wait_ge(v_done, 2 * g)
                for t in range(GT):
                    last = pe.matmul(v_ps[:, t * D:(t + 1) * D], hT[:, g * GT + t, :], col(attn_sb, ATTN, "wv"),
                                     start=True, stop=True)
                last.then_inc(v_mm, 1)

            def sum_kv(g):
                pe.wait_ge(k_done, g + 1)
                pe.wait_ge(v_done, 2 * g + 2)
                if g == GPB:
                    pe.wait_ge(q_done, GROUPS)
                for t in range(GT):
                    n = (g % GPB) * GT + t
                    last = pe.matmul(kv_ps[g // GPB][:, 0:D + 1], k_sb[:, g % 2, t, :], v_sb[:, g % 2, t, :],
                                     start=n == 0, stop=n == TPB - 1)
                last.then_inc(kv_mm, 1)

            pe.wait_ge(const_in, 16)
            transposes(0)
            pe.wait_ge(attn_in, 16)
            query(0)
            transposes(1)
            pe.wait_ge(bk_steps, 4)
            key(0)
            pe.wait_ge(hT_done, 1)
            transposes(2)
            value(0)
            def attend(g):
                b = g // GPB
                if g % GPB == 0:
                    pe.wait_ge(kv_done, 2 * b + 2)
                if g == 0:
                    pe.wait_ge(gated_done, 2)
                elif g == 2:
                    pe.wait_ge(k_done, GROUPS)
                    pe.wait_ge(v_done, 2 * GROUPS)
                else:
                    pe.wait_ge(att_done, min(g, 2))
                for t in range(GT):
                    last = pe.matmul(o_ps[g][:, t * 256:t * 256 + D + H], qT[:, g * GT + t, :], kv_heads[:, b, :],
                                     start=True, stop=True)
                last.then_inc(o_mm, 1)

            def turn_attention(g):
                pe.wait_ge(att_done, g + 1)
                pe.wait_ge(hT_done, GROUPS)
                if g:
                    pe.wait_ge(attT_done, g)
                for t in range(GT):
                    last = pe.transpose(attT_ps[:, t * P:(t + 1) * P], att[:, g % 2, t, :], ident)
                last.then_inc(attT_mm, 1)

            def project(g):
                pe.wait_ge(attT_done, g + 1)
                if g % 2 == 0:
                    pe.wait_ge(kvfull_done, g // 2 + 1)
                else:
                    pe.wait_ge(x1_done, g // 2 + 1)
                for t in range(GT):
                    last = pe.matmul(y_ps[g][:, t * D:(t + 1) * D], attT[:, g % 2, t, :], wo_gated[:, g // GPB, :],
                                     start=True, stop=True)
                last.then_inc(y_mm, 1)

            def route(g):
                pe.wait_ge(hT_done, GROUPS + g + 1)
                for t in range(GT):
                    last = pe.matmul(route_ps[g][:, t * E:(t + 1) * E], hT[:, g * GT + t, :], col(attn_sb, ATTN, "gate"),
                                     start=True, stop=True)
                last.then_inc(logit_mm, 1)

            def shared_gate(c, f):
                if c:
                    pe.wait_ge(sgelu_done, (c - 1) * FT + f + 1)
                pe.matmul(tiled(hid_ps[f]), wshared[:, f * P:(f + 1) * P], group(hT, c), start=True, stop=True).then_inc(sg_mm, 1)

            def shared_up(c, f):
                if c:
                    pe.wait_ge(sup_done, (c - 1) * FT + f + 1)
                pe.matmul(tiled(hid_ps[FT + f]), wshared[:, (FT + f) * P:(FT + f + 1) * P], group(hT, c),
                          start=True, stop=True).then_inc(su_mm, 1)

            def shared_down(c):
                pe.wait_ge(shid_done, (c + 1) * FT)
                for f in range(FT):
                    last = pe.matmul(acc[c], wshared[:, (2 * FT + f) * P:(2 * FT + f + 1) * P], hid_s[:, c % 2, f, :],
                                     start=f == 0, stop=False, skip_group_check=True)
                last.then_inc(sdown_mm, 1)

            query(1)
            key(1)
            pe.wait_ge(hT_done, 2)
            transposes(3)
            value(1)
            pe.wait_ge(gadiag_done, B)
            pe.matmul(ga_ps[:, 0:B * D], ones[:, 0:P], ga_diag[:, :, :].rearrange("p b d -> p (b d)"), start=True, stop=True)\
                .then_inc(ga_mm, 1)
            sum_kv(0)
            query(2)
            sum_kv(1)
            key(2)
            value(2)
            attend(0)
            query(3)
            key(3)
            turn_attention(0)
            attend(1)
            value(3)
            project(0)
            sum_kv(2)
            turn_attention(1)
            sum_kv(3)
            project(1)
            attend(2)
            attend(3)
            transposes(GROUPS)
            turn_attention(2)
            route(0)
            project(2)
            turn_attention(3)
            project(3)
            pe.wait_ge(att_done, GROUPS)
            pe.wait_ge(shared_in, 16)
            transposes(GROUPS + 1)
            shared_gate(0, 0)
            route(1)
            transposes(GROUPS + 2)
            shared_gate(0, 1)
            pe.wait_ge(shift_done, 1)
            transposes(GROUPS + 3)
            route(2)
            route(3)
            pe.wait_ge(score_done, B)
            for q in range(QUARTERS):
                last = pe.transpose(scoresT_ps[0:ROWS, q * P:(q + 1) * P], scores[:, q, :, :, :].rearrange("p h b e -> p (h b e)"), ident)
            last.then_inc(scoresT_mm, 1)

            pe.wait_ge(gbdiag_done, B)
            pe.wait_ge(attT_done, GROUPS)
            pe.matmul(gb_ps[:, 0:B * D], ones[:, 0:P], gb_diag[:, :, :].rearrange("p b d -> p (b d)"), start=True, stop=True)\
                .then_inc(gb_mm, 1)
            pe.wait_ge(shift_done, GROUPS - 1)
            shared_up(0, 0)
            shared_up(0, 1)
            for c in range(1, GROUPS):
                if c == 2:
                    pe.wait_ge(max_done, LATE_ROUND)
                for f in range(FT):
                    shared_gate(c, f)
                    shared_up(c, f)
                if c == 1:
                    pe.wait_ge(x1_done, GROUPS)
                if c == GROUPS - 1:
                    pe.wait_ge(gbrow_done, 1)
                shared_down(c - 1)

            pe.wait_ge(sup_done, GROUPS * FT)
            pe.wait_ge(wheref_done, 1)
            pe.transpose(merge_ps[:, 0:ROWS], best[:, :], ident[0:ROWS, 0:ROWS])
            pe.transpose(merge_ps[:, ROWS:2 * ROWS], wheref[:, :], ident[0:ROWS, 0:ROWS]).then_inc(lists_mm, 1)
            pe.wait_ge(merge_steps, LISTED)
            for k in range(2):
                last = pe.matmul(merge_ps[:, (4 + k) * BE:(5 + k) * BE], flip, lists[:, k, 1, :], start=True, stop=True)
            last.then_inc(flip_mm, 1)
            shared_down(GROUPS - 1)
            for _ in range(FILL):
                pe.matmul(gu_ps[0], ones[:, 0:P], ones[:, :], start=True, stop=True)

            def turn(p, u, first=False):
                pe.wait_ge(rows_in[x_slot(p, u)], (p[0] + 1) * 16)
                if not first:
                    pe.wait_ge(xeT_done, number(p) * UNITS + u)
                pe.transpose(xeT_ps[:, u * P:(u + 1) * P], xe[:, x_slot(p, u), :], ident).then_inc(xeT_mm, 1)

            def gate_up(p, u):
                if u % B == 0:
                    pe.wait_ge(w_in[w_slot(p, u)], (p[0] + 1) * 16)
                pe.wait_ge(xeT_done, number(p) * UNITS + u + 1)
                for j in range(2 * FT):
                    last = pe.matmul(gu_ps[u % 2][:, j * P:(j + 1) * P], wring[:, w_slot(p, u), j * P:(j + 1) * P], xeT[:, u, :],
                                     start=True, stop=True)
                last.then_inc(gu_mm, 1)

            def down(p, u):
                pe.wait_ge(hid_done, number(p) * UNITS + u + 1)
                if u or not same(p, FIRST):
                    q, v = (p, u - 1) if u else (before(p), UNITS - 1)
                    if by_product(q, v):
                        pe.wait_ge(hi_done, (products_before(q) * B + v % B + 1) * 2)
                    else:
                        pe.wait_ge(weighed_done, scatters_before(q, v) * B + v % B + 1)
                for f in range(FT):
                    last = pe.matmul(eo_ps[:, 0:D], hid_e[:, u, f, :],
                                     wring[:, w_slot(p, u), (2 * FT + f) * P:(2 * FT + f + 1) * P], start=f == 0, stop=f == FT - 1)
                last.then_inc(eo_mm, 1)

            def put_back(p, b):
                pe.wait_ge(lo_done, products_before(p) * B + b + 1)
                pe.wait_ge(back_done, products_before(p) * B + b + 1)
                for k, part in enumerate((eo_hi, eo_lo)):
                    for c in range(GPB):
                        last = pe.matmul(acc[b * GPB + c], part[:, b, :], back[:, b, c * GN:(c + 1) * GN],
                                         start=False, stop=same(p, LAST) and k == 1, skip_group_check=True)
                last.then_inc(back_mm, 1)

            def step(p, u):
                if u + 1 < UNITS:
                    turn(p, u + 1)
                elif not same(p, LAST):
                    turn(after(p), 0)
                gate_up(p, u)
                if u:
                    down(p, u - 1)
                elif not same(p, FIRST):
                    down(before(p), UNITS - 1)
                if u < B and not same(p, FIRST) and by_product(before(p), B):
                    put_back(before(p), u)

            pe.wait_ge(merge_steps, MERGED)
            turn(FIRST, 0, first=True)
            all_steps(pe, step)

            def token_major(g):
                for t in range(GT):
                    last = pe.transpose(room[g][:, t * P:(t + 1) * P], moeT[:, g, t * P:(t + 1) * P], ident)
                last.then_inc(moeT_mm, 1)

            put_back(LAST, 0)
            down(LAST, UNITS - 1)
            pe.wait_ge(hid_done, B * E)
            pe.wait_ge(moe_dve, 1)
            token_major(0)
            put_back(LAST, 1)
            for g in range(1, GROUPS):
                pe.wait_ge(moe_act, g)
                token_major(g)



def kernel(L0_attn_x, L0_attn_W_q, L0_attn_b_q, L0_attn_W_k, L0_attn_b_k, L0_attn_W_v, L0_attn_b_v, L0_attn_W_o,
           L0_attn_b_o, L0_ffn_gate_w, L0_ffn_Wg, L0_ffn_Wu, L0_ffn_Wd, L0_ffn_Ws_g, L0_ffn_Ws_u, L0_ffn_Ws_d, L0_c,
           L0_wmod):
    import numpy as np
    import concourse.bacc as bacc
    from concourse.bass_utils import run_bass_kernel_spmd

    f32 = np.float32

    def a(v):
        return np.asarray(v)

    def wide(v):
        return np.broadcast_to(a(v)[None, :], (P, D))

    early = np.concatenate([a(L0_c).T, a(L0_attn_b_q)[:, None], np.full((P, 1), LN_EPS, f32), a(L0_wmod)], axis=1)
    attn = np.concatenate([a(L0_attn_W_q).T, a(L0_attn_W_k).T, a(L0_attn_W_v).T, a(L0_attn_W_o).T,
                           wide(L0_attn_b_v), wide(L0_attn_b_o), a(L0_ffn_gate_w).T], axis=1)
    bk_row = np.concatenate([np.tile(a(L0_attn_b_k), (2, 1)), np.array([[1, 0], [-1, 1]], f32)], axis=1)

    eye = np.eye(P, dtype=f32)
    block_of = np.arange(P) // (D // H)
    decay = np.exp(-np.arange(N, dtype=f32) / N).astype(f32)
    const = np.concatenate([
        eye, eye[:, ::-1], (block_of[:, None] == block_of[None, :]).astype(f32),
        (block_of[:, None] == np.arange(H)[None, :]).astype(f32),
        decay.reshape(TPB, P).T, (f32(1e-6) / decay).astype(f32).reshape(TPB, P).T], axis=1)
    iota = np.tile(np.arange(N, dtype=f32), (P, 1))

    def expert_layout(wg, wu, wd):
        n = wg.shape[0]
        gate_up = np.concatenate([wg.transpose(0, 2, 1), wu.transpose(0, 2, 1)], axis=2)
        down = wd.transpose(0, 2, 1).reshape(n, FT, P, D).transpose(0, 2, 1, 3).reshape(n, P, FT * D)
        return np.concatenate([gate_up, down], axis=2)

    wexp = np.concatenate([expert_layout(a(L0_ffn_Wg), a(L0_ffn_Wu), a(L0_ffn_Wd)),
                           expert_layout(a(L0_ffn_Ws_g)[None], a(L0_ffn_Ws_u)[None], a(L0_ffn_Ws_d)[None])], axis=0)

    arrays = {"in_x": a(L0_attn_x), "in_early": early, "in_attn": attn, "in_bk_row": bk_row, "in_const": const,
              "in_iota": iota, "in_wexp": wexp}
    arrays = {k: np.ascontiguousarray(v) for k, v in arrays.items()}

    nc = bacc.Bacc("TRN2", target_bir_lowering=False, num_devices=1)
    args = [nc.dram_tensor(k, v.shape, F32, kind="ExternalInput").ap() for k, v in arrays.items()]
    args.append(nc.dram_tensor("out_y", (B, N, D), F32, kind="ExternalOutput").ap())
    adaln_moe_block(nc, *args)
    r = run_bass_kernel_spmd(nc, [arrays], core_ids=[0])
    return r.results[0]["out_y"]
```
